# Optimizing a Trainium2 kernel written in Bass

```python
import numpy as np
import jax
import jax.numpy as jnp

def _softmax(x, axis=-1):
    return jax.nn.softmax(x, axis=axis)

def _gelu(x):
    return jax.nn.gelu(x, approximate=True)

def _silu(x):
    return jax.nn.silu(x)

def _sigmoid(x):
    return jax.nn.sigmoid(x)

def _layernorm(x, axis=-1, eps=1e-05):
    m = jnp.mean(x, axis=axis, keepdims=True)
    v = jnp.var(x, axis=axis, keepdims=True)
    return (x - m) / jnp.sqrt(v + eps)

def _scatter_add(tgt, idx, src, axis=0):
    return tgt.at[idx].add(src)

def _segment_sum(src, seg, n):
    return jax.ops.segment_sum(src, seg, n)
kernel_name = 'mk_metaformer_d2_conv_nchw512_r4_e0ccdc'

def setup_inputs(seed: int=0):
    np.random.seed(seed)
    _w = jnp.asarray

    def _rec_inputs():
        import jax
        import jax.numpy as jnp
        _gk = jax.random.key(seed)
        x = -0.0001329 + 0.9999 * jax.random.normal(jax.random.fold_in(_gk, 1), (16, 128, 24, 24), jnp.float32)
        return x
    x = _rec_inputs()

    def _L0_conv_setup():
        import jax, jax.numpy as jnp
        import numpy as np
        from jax import lax
        DW_HASH_CH = 1337
        DW_HASH_KH = 7919
        DW_HASH_KW = 2971
        DW_HASH_LAYER = 104729
        SIGN_HASH_A = 4099
        SIGN_HASH_B = 6151
        SIGN_HASH_C = 14887
        CHANNELS = 128
        KH, KW = (7, 7)
        CODEBOOK_SIZE = 1024
        LAYER_ID = 3
        STRIDE = (1, 1)
        PADDING = ((3, 3), (3, 3))

        def _hash_tables():
            ch = np.arange(CHANNELS).reshape(CHANNELS, 1, 1)
            kh = np.arange(KH).reshape(1, KH, 1)
            kw = np.arange(KW).reshape(1, 1, KW)
            idx = (ch * DW_HASH_CH + kh * DW_HASH_KH + kw * DW_HASH_KW + LAYER_ID * DW_HASH_LAYER) % CODEBOOK_SIZE
            bits = (ch * SIGN_HASH_A + kh * SIGN_HASH_B + kw * SIGN_HASH_C + LAYER_ID * (SIGN_HASH_A + 29)) % 2
            signs = bits.astype(np.float32) * 2.0 - 1.0
            return (jnp.asarray(idx), jnp.asarray(signs))
        _IDX, _SIGNS = _hash_tables()
        key = jax.random.key(seed)
        k1, k2 = jax.random.split(key)
        x = jax.random.normal(k1, (16, CHANNELS, 24, 24), dtype=jnp.float32)
        codebook = jax.random.normal(k2, (CODEBOOK_SIZE,), dtype=jnp.float32) * 0.01
        bias = jnp.zeros((CHANNELS,), dtype=jnp.float32)
        return {'x': x, 'codebook': codebook, 'bias': bias}
    _L0_conv_all = _L0_conv_setup()
    _L0_conv_in = {k: v for k, v in _L0_conv_all.items() if k in ('codebook', 'bias')}
    del _L0_conv_all

    def _L0_ffn_setup():
        import jax, jax.numpy as jnp
        import numpy as np
        D_MODEL = 128
        D_FF = 512
        NUM_EXPERTS = 8
        TOP_K = 2
        key = jax.random.key(seed)
        k_x, k_g, k_w1, k_w2 = jax.random.split(key, 4)
        x = jax.random.normal(k_x, (8, 1024, D_MODEL), dtype=jnp.float32)
        Wg = jax.random.normal(k_g, (D_MODEL, NUM_EXPERTS), dtype=jnp.float32) * (1.0 / np.sqrt(D_MODEL))
        W1 = jax.random.normal(k_w1, (NUM_EXPERTS, D_MODEL, D_FF), dtype=jnp.float32) * (1.0 / np.sqrt(D_MODEL))
        W2 = jax.random.normal(k_w2, (NUM_EXPERTS, D_FF, D_MODEL), dtype=jnp.float32) * (1.0 / np.sqrt(D_FF))
        return {'x': x, 'Wg': Wg, 'W1': W1, 'W2': W2}
    _L0_ffn_all = _L0_ffn_setup()
    _L0_ffn_in = {k: v for k, v in _L0_ffn_all.items() if k in ('Wg', 'W1', 'W2')}
    del _L0_ffn_all

    def _L1_conv_setup():
        import jax, jax.numpy as jnp
        from jax import lax
        import numpy as np
        UP = 2
        DOWN = 2
        PADDING = (11, 10, 11, 10)
        GAIN = float(np.sqrt(2.0))
        SLOPE = 0.2
        CLAMP = 256.0
        UP_TAPS = 12
        IN_CUTOFF = 8.0
        OUT_CUTOFF = 8.0
        IN_HALF_WIDTH = 6.0
        OUT_HALF_WIDTH = 6.0
        TEMP_FS = 32.0

        def _design_lowpass(numtaps, cutoff, width, fs):
            nyq = fs / 2.0
            atten = 2.285 * (numtaps - 1) * np.pi * (width / nyq) + 7.95
            if atten > 50.0:
                beta = 0.1102 * (atten - 8.7)
            elif atten > 21.0:
                beta = 0.5842 * (atten - 21.0) ** 0.4 + 0.07886 * (atten - 21.0)
            else:
                beta = 0.0
            m = np.arange(numtaps) - (numtaps - 1) / 2.0
            c = cutoff / nyq
            h = c * np.sinc(c * m)
            h = h * np.kaiser(numtaps, beta)
            h = h / np.sum(h)
            return h.astype(np.float32)

        def _upfirdn2d_sep(x, f, up, down, pad, gain):
            N, C, H, W = x.shape
            fr = f[::-1].astype(x.dtype)
            kH = fr.reshape(1, 1, -1, 1)
            kW = fr.reshape(1, 1, 1, -1)
            px0, px1, py0, py1 = pad
            xr = x.reshape(N * C, 1, H, W)
            xr = lax.conv_general_dilated(xr, kH, window_strides=(down, 1), padding=((py0, py1 + up - 1), (0, 0)), lhs_dilation=(up, 1))
            xr = lax.conv_general_dilated(xr, kW, window_strides=(1, down), padding=((0, 0), (px0, px1 + up - 1)), lhs_dilation=(1, up))
            Ho, Wo = (xr.shape[2], xr.shape[3])
            return xr.reshape(N, C, Ho, Wo) * gain
        key = jax.random.key(seed)
        k1, k2 = jax.random.split(key)
        x = jax.random.normal(k1, (8, 128, 16, 16), dtype=jnp.float32)
        bias = jax.random.normal(k2, (128,), dtype=jnp.float32) * 0.1
        up_filter = jnp.asarray(_design_lowpass(UP_TAPS, IN_CUTOFF, IN_HALF_WIDTH * 2, TEMP_FS))
        down_filter = jnp.asarray(_design_lowpass(UP_TAPS, OUT_CUTOFF, OUT_HALF_WIDTH * 2, TEMP_FS))
        return {'x': x, 'bias': bias, 'up_filter': up_filter, 'down_filter': down_filter}
    _L1_conv_all = _L1_conv_setup()
    _L1_conv_in = {k: v for k, v in _L1_conv_all.items() if k in ('bias', 'up_filter', 'down_filter')}
    del _L1_conv_all

    def _L1_ffn_setup():
        import jax, jax.numpy as jnp
        import numpy as np
        TOP_K = 2
        key = jax.random.key(seed)
        k0, k1, k2, k3, k4 = jax.random.split(key, 5)
        B, S, D, F, E = (1, 512, 128, 256, 8)
        scale = 0.02
        hidden_states = jax.random.normal(k0, (B, S, D), dtype=jnp.float32)
        router_w = jax.random.normal(k1, (D, E), dtype=jnp.float32) * scale
        w1 = jax.random.normal(k2, (E, D, F), dtype=jnp.float32) * scale
        w2 = jax.random.normal(k3, (E, F, D), dtype=jnp.float32) * scale
        w3 = jax.random.normal(k4, (E, D, F), dtype=jnp.float32) * scale
        return {'hidden_states': hidden_states, 'router_w': router_w, 'w1': w1, 'w2': w2, 'w3': w3}
    _L1_ffn_all = _L1_ffn_setup()
    _L1_ffn_in = {k: v for k, v in _L1_ffn_all.items() if k in ('router_w', 'w1', 'w2', 'w3')}
    del _L1_ffn_all
    return {'x': x, 'L0_conv_codebook': _L0_conv_in['codebook'], 'L0_conv_bias': _L0_conv_in['bias'], 'L0_ffn_Wg': _L0_ffn_in['Wg'], 'L0_ffn_W1': _L0_ffn_in['W1'], 'L0_ffn_W2': _L0_ffn_in['W2'], 'L1_conv_bias': _L1_conv_in['bias'], 'L1_conv_up_filter': _L1_conv_in['up_filter'], 'L1_conv_down_filter': _L1_conv_in['down_filter'], 'L1_ffn_router_w': _L1_ffn_in['router_w'], 'L1_ffn_w1': _L1_ffn_in['w1'], 'L1_ffn_w2': _L1_ffn_in['w2'], 'L1_ffn_w3': _L1_ffn_in['w3']}

def reference(x, L0_conv_codebook, L0_conv_bias, L0_ffn_Wg, L0_ffn_W1, L0_ffn_W2, L1_conv_bias, L1_conv_up_filter, L1_conv_down_filter, L1_ffn_router_w, L1_ffn_w1, L1_ffn_w2, L1_ffn_w3):
    import jax
    import jax.numpy as jnp

    def _L0_conv_ref(x, codebook, bias):
        import jax, jax.numpy as jnp
        import numpy as np
        from jax import lax
        DW_HASH_CH = 1337
        DW_HASH_KH = 7919
        DW_HASH_KW = 2971
        DW_HASH_LAYER = 104729
        SIGN_HASH_A = 4099
        SIGN_HASH_B = 6151
        SIGN_HASH_C = 14887
        CHANNELS = 128
        KH, KW = (7, 7)
        CODEBOOK_SIZE = 1024
        LAYER_ID = 3
        STRIDE = (1, 1)
        PADDING = ((3, 3), (3, 3))

        def _hash_tables():
            ch = np.arange(CHANNELS).reshape(CHANNELS, 1, 1)
            kh = np.arange(KH).reshape(1, KH, 1)
            kw = np.arange(KW).reshape(1, 1, KW)
            idx = (ch * DW_HASH_CH + kh * DW_HASH_KH + kw * DW_HASH_KW + LAYER_ID * DW_HASH_LAYER) % CODEBOOK_SIZE
            bits = (ch * SIGN_HASH_A + kh * SIGN_HASH_B + kw * SIGN_HASH_C + LAYER_ID * (SIGN_HASH_A + 29)) % 2
            signs = bits.astype(np.float32) * 2.0 - 1.0
            return (jnp.asarray(idx), jnp.asarray(signs))
        _IDX, _SIGNS = _hash_tables()
        weight = codebook[_IDX] * _SIGNS.astype(codebook.dtype)
        weight = weight[:, None, :, :]
        out = lax.conv_general_dilated(x, weight, window_strides=STRIDE, padding=PADDING, dimension_numbers=('NCHW', 'OIHW', 'NCHW'), feature_group_count=CHANNELS)
        return out + bias[None, :, None, None]

    def _L0_ffn_ref(x, Wg, W1, W2):
        import jax, jax.numpy as jnp
        import numpy as np
        D_MODEL = 128
        D_FF = 512
        NUM_EXPERTS = 8
        TOP_K = 2
        B, S, D = x.shape
        E = Wg.shape[-1]
        router_logits = jnp.einsum('bsd,de->bse', x, Wg)
        top_logits, top_idx = jax.lax.top_k(router_logits, TOP_K)
        top_w = jax.nn.softmax(top_logits, axis=-1)
        combine = jnp.sum(jax.nn.one_hot(top_idx, E, dtype=x.dtype) * top_w[..., None], axis=-2)
        xt = x.reshape(B * S, D)
        cw = combine.reshape(B * S, E)
        out = jnp.zeros_like(xt)
        for e in range(E):
            h = jax.nn.silu(xt @ W1[e]) @ W2[e]
            out = out + cw[:, e:e + 1] * h
        return out.reshape(B, S, D)

    def _L1_conv_ref(x, bias, up_filter, down_filter):
        import jax, jax.numpy as jnp
        from jax import lax
        import numpy as np
        UP = 2
        DOWN = 2
        PADDING = (11, 10, 11, 10)
        GAIN = float(np.sqrt(2.0))
        SLOPE = 0.2
        CLAMP = 256.0
        UP_TAPS = 12
        IN_CUTOFF = 8.0
        OUT_CUTOFF = 8.0
        IN_HALF_WIDTH = 6.0
        OUT_HALF_WIDTH = 6.0
        TEMP_FS = 32.0

        def _design_lowpass(numtaps, cutoff, width, fs):
            nyq = fs / 2.0
            atten = 2.285 * (numtaps - 1) * np.pi * (width / nyq) + 7.95
            if atten > 50.0:
                beta = 0.1102 * (atten - 8.7)
            elif atten > 21.0:
                beta = 0.5842 * (atten - 21.0) ** 0.4 + 0.07886 * (atten - 21.0)
            else:
                beta = 0.0
            m = np.arange(numtaps) - (numtaps - 1) / 2.0
            c = cutoff / nyq
            h = c * np.sinc(c * m)
            h = h * np.kaiser(numtaps, beta)
            h = h / np.sum(h)
            return h.astype(np.float32)

        def _upfirdn2d_sep(x, f, up, down, pad, gain):
            N, C, H, W = x.shape
            fr = f[::-1].astype(x.dtype)
            kH = fr.reshape(1, 1, -1, 1)
            kW = fr.reshape(1, 1, 1, -1)
            px0, px1, py0, py1 = pad
            xr = x.reshape(N * C, 1, H, W)
            xr = lax.conv_general_dilated(xr, kH, window_strides=(down, 1), padding=((py0, py1 + up - 1), (0, 0)), lhs_dilation=(up, 1))
            xr = lax.conv_general_dilated(xr, kW, window_strides=(1, down), padding=((0, 0), (px0, px1 + up - 1)), lhs_dilation=(1, up))
            Ho, Wo = (xr.shape[2], xr.shape[3])
            return xr.reshape(N, C, Ho, Wo) * gain
        y = _upfirdn2d_sep(x, up_filter, UP, 1, PADDING, float(UP * UP))
        y = y + bias[None, :, None, None]
        y = jnp.where(y >= 0, y, y * SLOPE) * GAIN
        y = jnp.clip(y, -CLAMP, CLAMP)
        y = _upfirdn2d_sep(y, down_filter, 1, DOWN, (0, 0, 0, 0), 1.0)
        return y

    def _L1_ffn_ref(hidden_states, router_w, w1, w2, w3):
        import jax, jax.numpy as jnp
        import numpy as np
        TOP_K = 2
        B, S, D = hidden_states.shape
        E = router_w.shape[1]
        x = hidden_states.reshape(-1, D)
        T = x.shape[0]
        router_logits = x @ router_w
        probs = jax.nn.softmax(router_logits.astype(jnp.float32), axis=-1)
        routing_weights, selected_experts = jax.lax.top_k(probs, TOP_K)
        routing_weights = routing_weights / routing_weights.sum(axis=-1, keepdims=True)
        routing_weights = routing_weights.astype(x.dtype)
        combine = jnp.zeros((T, E), dtype=x.dtype).at[jnp.arange(T)[:, None], selected_experts].add(routing_weights)
        gate = jax.nn.silu(jnp.einsum('td,edf->tef', x, w1))
        up = jnp.einsum('td,edf->tef', x, w3)
        h = gate * up * combine[:, :, None]
        out = jnp.einsum('tef,efd->td', h, w2)
        return out.reshape(B, S, D)

    def _gn(v, G=32, eps=1e-05):
        B_, C_, H_, W_ = v.shape
        g = v.reshape(B_, G, C_ // G, H_, W_)
        m = jnp.mean(g, axis=(2, 3, 4), keepdims=True)
        s = jnp.var(g, axis=(2, 3, 4), keepdims=True)
        return ((g - m) / jnp.sqrt(s + eps)).reshape(v.shape)

    def _ln_c(v, eps=1e-06):
        m = jnp.mean(v, axis=1, keepdims=True)
        s = jnp.var(v, axis=1, keepdims=True)
        return (v - m) / jnp.sqrt(s + eps)

    def _ln_t(v, eps=1e-05):
        m = jnp.mean(v, axis=-1, keepdims=True)
        s = jnp.var(v, axis=-1, keepdims=True)
        return (v - m) / jnp.sqrt(s + eps)

    def _to_tokens(v):
        B_, C_, H_, W_ = v.shape
        return v.reshape(B_, C_, H_ * W_).transpose(0, 2, 1)

    def _from_tokens(t, like):
        B_, C_, H_, W_ = like.shape
        return t.transpose(0, 2, 1).reshape(B_, C_, H_, W_)
    x = x + _L0_conv_ref(_ln_c(x), L0_conv_codebook, L0_conv_bias)
    t = _to_tokens(x)
    t = t + _L0_ffn_ref(_ln_t(t), L0_ffn_Wg, L0_ffn_W1, L0_ffn_W2)
    x = _from_tokens(t, x)
    x = x + _L1_conv_ref(_ln_c(x), L1_conv_bias, L1_conv_up_filter, L1_conv_down_filter)
    t = _to_tokens(x)
    t = t + _L1_ffn_ref(_ln_t(t), L1_ffn_router_w, L1_ffn_w1, L1_ffn_w2, L1_ffn_w3)
    x = _from_tokens(t, x)
    return x

_drawn_inputs = setup_inputs


def setup_inputs(seed=0):
    import zlib

    import numpy as np

    out = dict(_drawn_inputs(seed))
    spreads = {'L0_conv_bias': (0.0, 0.1)}
    factors = {'L1_ffn_router_w': 8.0, 'L1_ffn_w1': 8.0, 'L1_ffn_w2': 8.0, 'L1_ffn_w3': 8.0}
    for name, (base, spread) in spreads.items():
        noise = np.random.default_rng([zlib.crc32(name.encode()), seed]).standard_normal(out[name].shape)
        drawn = base * np.exp(spread * noise) if base else spread * noise
        out[name] = jnp.asarray(drawn.astype(out[name].dtype))
    for name, factor in factors.items():
        out[name] = (out[name] * factor).astype(out[name].dtype)
    return out
```

```python
from contextlib import ExitStack, contextmanager

import numpy as np

import concourse.bass as bass
from concourse import mybir

F32 = mybir.dt.float32
F32R = mybir.dt.float32r
I32 = mybir.dt.int32
U32 = mybir.dt.uint32
ALU = mybir.AluOpType
ACT = mybir.ActivationFunctionType
AX = mybir.AxisListType

P = 128
IMAGES, SIDE = 16, 24
PIXELS = SIDE * SIDE
TOKENS = IMAGES * PIXELS
TILES = TOKENS // P
GT = 4
GROUPS = TILES // GT
EXPERTS = 8
FF = 512
BLOCKS = 2 * TILES + EXPERTS
TABLE = BLOCKS + 8
REGION = TOKENS + P

CGS, CIN, RPAD = 4, 32, 32
TAPS, HALO = 7, 3
WPAD = SIDE + 2 * HALO
NW = IMAGES * SIDE
KLEN = TAPS * P
WRING = 4

FIR = 12
ROWS = 5
TPX = ROWS * SIDE
QT = 5
UP = 58
PAIRS = UP // 2
PPX = 2 * UP
IG = 4
NC = IG * P
IMAGE_GROUPS = IMAGES // IG
N_UP = 2 * ROWS + 4
N_DOWN = 2 * ROWS


@contextmanager
def stage_semaphores(nc, prefix):
    taken = []

    def named(name):
        taken.append(nc.alloc_semaphore(name=prefix + name))
        return taken[-1]

    yield named
    nc.clear_and_free_semaphores(taken)
    nc.all_engine_barrier()


class Chain:

    def __init__(self, eng, sem, base=0):
        self.eng, self.sem, self.base, self.n = eng, sem, base, 0

    def after(self, ins, beat=None):
        ins.then_inc(self.sem, 1)
        self.n += 1
        self.eng.wait_ge(self.sem, self.base + self.n)
        if beat is not None:
            self.eng.sem_inc(beat, 1)


def conv0_phase(nc, io, x1d):
    with ExitStack() as ctx:
        sb = lambda n, s, d=F32: ctx.enter_context(nc.sbuf_tensor(n, s, d))
        sem = ctx.enter_context(stage_semaphores(nc, ""))
        x = sb("c0_x", [P, NW, CIN])
        pad = sb("c0_pad", [P, CIN, IMAGES, WPAD])
        sq = sb("c0_sq", [P, NW, CIN])
        part = sb("c0_part", [P, 2, NW])
        rstd = sb("c0_rstd", [P, NW])
        wring = sb("c0_w", [P, WRING, KLEN])
        tmp = sb("c0_tmp", [P, 2, NW])
        bias = sb("c0_bias", [P, CIN])
        mean_w = sb("c0_meanw", [P, P])
        check = sb("c0_check", [P, 2, NW])
        osign = sb("c0_osign", [P, 2])
        ps_stat = [ctx.enter_context(nc.psum_tensor(f"c0_ps{i}", [P, 512], F32)) for i in range(4)]
        ps = [ctx.enter_context(nc.psum_tensor(f"c0_acc{i}", [P, 512], F32)) for i in range(4)]
        consts_in, x_in = sem("c0_consts_in"), [sem(f"c0_x_in{i}") for i in range(4)]
        w_in = [sem(f"c0_w_in{i}") for i in range(WRING)]
        padded, sums, mean_ready, centred = sem("c0_padded"), sem("c0_sums"), sem("c0_mean"), sem("c0_centred")
        var_ready, std_ready = sem("c0_var_ready"), sem("c0_std_ready")
        squared, chain, normed = sem("c0_squared"), sem("c0_chain"), sem("c0_normed")
        acc_ready, acc_free, x1_ready, stored = sem("c0_acc_ready"), sem("c0_acc_free"), sem("c0_x1_ready"), sem("c0_stored")
        Q = NW // 4
        block = ctx.enter_context(nc.Block())

        def store(eng, cg):
            eng.wait_ge(x1_ready, CIN)
            for n in range(IMAGES):
                eng.dma_start(
                    x1d[n * PIXELS:(n + 1) * PIXELS, cg * CIN:(cg + 1) * CIN].rearrange("(h w) c -> h w c", w=SIDE),
                    x[cg * RPAD:cg * RPAD + SIDE, n * SIDE:(n + 1) * SIDE, :]).then_inc(stored, 16)

        @block.sync
        def _(sp):
            for q in range(4):
                sp.dma_start(x[:, q * Q:(q + 1) * Q, :], io["xh"][:, q * Q:(q + 1) * Q, :]).then_inc(x_in[q], 16)
            with sp.Fori(0, CIN // WRING) as it:
                for s in range(WRING):
                    sp.wait_ge(acc_free, WRING * it + s + 1)
                    sp.dma_start(wring[:, s, :], io["w0"][bass.ds(WRING * it + s, 1)].rearrange("a p k -> p (a k)")
                                 ).then_inc(w_in[s], 16)
            store(sp, 0)
            store(sp, 1)
            sp.wait_ge(stored, 16 * IMAGES * CGS)

        @block.gpsimd
        def _(pool):
            nc.gpsimd.memset(pad[:, :, :, 0:HALO], 0.0).then_inc(padded, 1)
            nc.gpsimd.memset(pad[:, :, :, HALO + SIDE:], 0.0).then_inc(padded, 1)

        @block.scalar
        def _(act):
            for dst, name in ((bias[:], "bias0"), (mean_w[:], "mean_w"), (check[:], "check"), (osign[:], "osign")):
                act.dma_start(dst, io[name]).then_inc(consts_in, 16)
            for q in range(4):
                act.wait_ge(centred, q + 1)
                src = pad[:, :, 4 * q:4 * q + 4, HALO:HALO + SIDE].rearrange("p c n w -> p n w c")
                for k in range(4):
                    ins = nc.scalar.activation(sq[:, q * Q + k * SIDE:q * Q + (k + 1) * SIDE, :], src[:, k], ACT.Square)
                ins.then_inc(squared, 1)
            for q in range(4):
                act.wait_ge(var_ready, q + 1)
                cols = slice(q * Q, (q + 1) * Q)
                nc.scalar.activation(rstd[:, cols], rstd[:, cols], ACT.Sqrt).then_inc(std_ready, 1)
            store(act, 2)
            store(act, 3)

        @block.tensor
        def _(pe):
            pe.wait_ge(consts_in, 64)
            for q in range(8):
                pe.wait_ge(sums, q + 1)
                k = q % 4
                nc.tensor.matmul(ps_stat[k][:, 0:Q], mean_w[:], part[:, q // 4, k * Q:(k + 1) * Q],
                                 start=True, stop=True).then_inc(mean_ready, 1)
            pe.wait_ge(normed, 4)
            pe.wait_ge(padded, 2)
            with pe.Fori(0, CIN // WRING) as it:
                for s in range(WRING):
                    pe.wait_ge(w_in[s], 16 * it + 16)
                    pe.wait_ge(acc_free, WRING * it + s + 1)
                    for kw in range(TAPS):
                        ins = nc.tensor.matmul(ps[s][:, 0:NW], wring[:, s, kw * P:(kw + 1) * P],
                                               pad[:, bass.ds(WRING * it + s, 1), :, kw:kw + SIDE].rearrange("p a n w -> p (a n) w"),
                                               start=kw == 0, stop=kw == TAPS - 1)
                    ins.then_inc(acc_ready, 1)

        @block.vector
        def _(dve):
            dve.sem_inc(acc_free, WRING)
            ch = Chain(dve, chain)
            dve.wait_ge(consts_in, 64)
            for q in range(4):
                cols = slice(q * Q, (q + 1) * Q)
                dve.wait_ge(x_in[q], 16)
                nc.vector.tensor_reduce(part[:, 0, cols], x[:, cols, :], AX.X, ALU.add).then_inc(sums, 1)
            for q in range(4):
                cols = slice(q * Q, (q + 1) * Q)
                dve.wait_ge(mean_ready, q + 1)
                for k in range(4):
                    c = slice(q * Q + k * SIDE, q * Q + (k + 1) * SIDE)
                    ins = nc.vector.tensor_tensor(
                        pad[:, :, 4 * q + k, HALO:HALO + SIDE].rearrange("p c w -> p w c"), x[:, c, :],
                        ps_stat[q][:, k * SIDE:(k + 1) * SIDE].unsqueeze(2).to_broadcast([P, SIDE, CIN]), ALU.subtract)
                ins.then_inc(centred, 1)
            for q in range(4):
                cols = slice(q * Q, (q + 1) * Q)
                dve.wait_ge(squared, q + 1)
                nc.vector.tensor_reduce(part[:, 1, cols], sq[:, cols, :], AX.X, ALU.add).then_inc(sums, 1)
            for q in range(4):
                cols = slice(q * Q, (q + 1) * Q)
                dve.wait_ge(mean_ready, 5 + q)
                nc.vector.tensor_scalar(rstd[:, cols], ps_stat[q][:, 0:Q], 1e-6, None, ALU.add).then_inc(var_ready, 1)
            for q in range(4):
                cols = slice(q * Q, (q + 1) * Q)
                dve.wait_ge(std_ready, q + 1)
                ch.after(nc.vector.reciprocal(rstd[:, cols], rstd[:, cols]))
                ch.after(nc.vector.tensor_tensor(rstd[:, cols], rstd[:, cols], check[:, 0, cols], ALU.mult))
                for k in range(4):
                    n = 4 * q + k
                    v = pad[:, :, n, HALO:HALO + SIDE]
                    ins = nc.vector.tensor_tensor(
                        v, v, rstd[:, n * SIDE:(n + 1) * SIDE].unsqueeze(1).to_broadcast([P, CIN, SIDE]), ALU.mult)
                ins.then_inc(normed, 1)
            base = ch.n
            with dve.Fori(0, CIN // WRING) as it:
                step = Chain(dve, chain, base + 2 * WRING * it)
                for s in range(WRING):
                    dve.wait_ge(acc_ready, WRING * it + s + 1)
                    ins = nc.vector.scalar_tensor_tensor(tmp[:, s % 2, :], ps[s][:, 0:NW], osign[:, s % 2:s % 2 + 1], check[:, 1, :],
                                                         ALU.mult, ALU.mult)
                    step.after(ins)
                    dve.sem_inc(acc_free, 1)
                    xr = x[:, :, bass.ds(WRING * it + s, 1)].rearrange("p n a -> p (n a)")
                    step.after(nc.vector.scalar_tensor_tensor(xr, tmp[:, s % 2, :], bias[:, bass.ds(WRING * it + s, 1)], xr,
                                                              ALU.add, ALU.add))
                    dve.sem_inc(x1_ready, 1)


class Routing:

    def __init__(self, nc, ctx):
        sb = lambda n, s, d=F32: ctx.enter_context(nc.sbuf_tensor(n, s, d))
        self.ident = sb("ident", [P, P])
        self.before = sb("before", [P, P])
        self.ones = sb("ones", [P, P])
        self.zeros = sb("zeros", [P, P])
        self.iota8 = sb("iota8", [P, 2 * GT, EXPERTS])
        self.region = sb("region", [P, GT * EXPERTS])
        self.tail = sb("tail", [P, EXPERTS])
        self.block_no = sb("block_no", [1, TABLE, EXPERTS])
        self.wg = sb("wg", [P, EXPERTS])
        self.slots_f = sb("slots_f", [P, TILES * 2])
        self.slots = sb("slots", [P, TILES * 2], I32)
        self.gap = sb("gap", [P, TILES])
        self.weight = sb("weight", [P, TILES, 2])
        self.table = sb("table", [1, 2, TABLE], I32)


class ExpertWeights:

    def __init__(self, nc, ctx, layer):
        sb = lambda n, d=F32: ctx.enter_context(nc.sbuf_tensor(f"{n}_{layer}", [P, EXPERTS * FF], d))
        self.w1f, self.w1h, self.w1l, self.w2 = sb("w1f"), sb("w1h", F32R), sb("w1l", F32R), sb("w2")


def route_phase(nc, io, r, wt, layer, xs, src, conv_out=None, x_out=None):
    with ExitStack() as ctx:
        sb = lambda n, s, d=F32: ctx.enter_context(nc.sbuf_tensor(f"r{layer}_{n}", s, d))
        sem = ctx.enter_context(stage_semaphores(nc, f"r{layer}_"))
        B = 3
        xt = sb("xt", [P, B, GT, P])
        zt = sb("zt", [P, B, GT, P]) if conv_out is not None else None
        xn = sb("xn", [P, B, GT, P])
        xnt = sb("xnt", [P, B, GT * P])
        stats, mv, rstd = sb("stats", [P, GT, 6]), sb("mv", [P, GT, 2]), sb("rstd", [P, GT])
        top, top_at = sb("top", [P, GT, 8]), sb("top_at", [P, GT, 8], U32)
        at = sb("at", [P, GT * 2])
        onehot = sb("onehot", [P, B, GT, 2, EXPERTS])
        picked = sb("picked", [P, B, GT, EXPERTS])
        before_group = sb("before_group", [P, B, EXPERTS])
        group_sum = sb("group_sum", [P, EXPERTS])
        rank, prod, slot_f = sb("rank", [P, GT * EXPERTS]), sb("prod", [P, GT, 2, EXPERTS]), sb("slot_f", [P, GT * 2])
        slot = sb("slot", [P, B, GT * 2], I32)
        count, tail_i = sb("count", [P, EXPERTS]), sb("tail_i", [P, EXPERTS], I32)
        nblk_i, nblk, upto = sb("nblk_i", [P, EXPERTS], I32), sb("nblk", [P, EXPERTS]), sb("upto", [P, EXPERTS])
        closer, moved, out_slot = sb("closer", [P, EXPERTS]), sb("moved", [P, 2 * TILES]), sb("out_slot", [P, 2 * TILES])
        passed, passed_n = sb("passed", [1, TABLE, EXPERTS]), sb("passed_n", [1, TABLE, EXPERTS])
        t_e, t_prev, t_j, t_m, t_f = (sb(f"tab{i}", [1, TABLE]) for i in range(5))
        ex = sb("ex", [P, TILES])
        ps = lambda n: ctx.enter_context(nc.psum_tensor(f"r{layer}_ps_{n}", [P, 512], F32))
        ps_t, ps_l, ps_rank = [ps(f"t{i}") for i in range(B)], [ps(f"l{i}") for i in range(B)], ps("rank")
        consts_in, w_in, w_split = sem("consts_in"), sem("w_in"), sem("w_split")
        x_in = [sem(f"x_in{b}") for b in range(B)]
        scattered = [sem(f"scattered{b}") for b in range(B)]
        chain, init = sem("chain"), sem("init")
        var_ready, std_ready, xn_ready, turned, xnt_ready = (sem(n) for n in ("var", "std", "xn", "turned", "xnt"))
        logits_ready, picked_ready, rank_ready, slot_ready = (sem(n) for n in ("logits", "picked", "rank", "slot"))
        total_ready, counted, tail_ready, tails, gap_ready, exp_ready = (
            sem(n) for n in ("total", "counted", "tail", "tails", "gap", "exp"))
        xsum_ready = sem("xsum")
        beat, pool_beat, sp_beat = sem("beat"), sem("pool_beat"), sem("sp_beat")
        stored = [sem(f"stored{b}") for b in range(B)]
        block = ctx.enter_context(nc.Block())
        LOADS = 2 if conv_out is not None else 1
        rows = lambda dram, g: dram[bass.ds(g * GT * P, GT * P), :].rearrange("(t p) c -> p t c", p=P)

        def groups(eng, step):
            for b in range(B):
                step(0, b, True)
            with eng.Fori(1, GROUPS // B) as it:
                for b in range(B):
                    step(it, b, False)

        @block.sync
        def _(sp):
            def load(it, b, first):
                if not first:
                    sp.wait_ge(xn_ready, B * it + b - B + 1)
                    if conv_out is not None:
                        sp.sem_inc(sp_beat, 1)
                        sp.wait_ge(stored[b], 16 * it)
                sp.dma_start(xt[:, b], rows(src, B * it + b)).then_inc(x_in[b], 16)
                if conv_out is not None:
                    sp.dma_start(zt[:, b], rows(conv_out, B * it + b)).then_inc(x_in[b], 16)
            groups(sp, load)

        @block.scalar
        def _(act):
            act.dma_start(r.wg[:], io[f"wg{layer}"]).then_inc(consts_in, 16)
            n_consts = 16
            if layer == 0:
                for dst, name in ((r.ident, "ident"), (r.before, "before"), (r.region, "region"), (r.tail, "tail")):
                    act.dma_start(dst[:], io[name]).then_inc(consts_in, 16)
                act.dma_start(r.iota8[:].rearrange("p a e -> p (a e)"), io["iota8"]).then_inc(consts_in, 16)
                act.dma_start(r.block_no[:].rearrange("p a e -> p (a e)"), io["block_no"]).then_inc(consts_in, 16)
            act.dma_start(wt.w1f[:], io[f"w1_{layer}"].rearrange("p e f -> p (e f)")).then_inc(w_in, 16)
            k2 = FF // P if layer == 0 else FF // P // 2
            act.dma_start(wt.w2[:].rearrange("p (e k) -> p e k", e=EXPERTS)[:, :, 0:k2 * P],
                          io[f"w2_{layer}"].rearrange("p e c d -> p e (c d)")).then_inc(w_in, 16)
            act.wait_ge(w_in, 32)

            def step(it, b, first):
                act.wait_ge(var_ready, B * it + b + 1)
                nc.scalar.activation(rstd[:], rstd[:], ACT.Sqrt).then_inc(std_ready, 1)
                if conv_out is not None:
                    act.wait_ge(xsum_ready, B * it + b + 1)
                    act.dma_start(rows(x_out, B * it + b), xt[:, b]).then_inc(stored[b], 16)
                act.wait_ge(turned, B * it + b + 1)
                nc.scalar.activation(xnt[:, b], ps_t[b][:], ACT.Copy).then_inc(xnt_ready, 1)
            groups(act, step)
            nc.scalar.activation(wt.w1h[:], wt.w1f[:], ACT.Copy).then_inc(w_split, 1)
            act.wait_ge(gap_ready, 1)
            nc.scalar.activation(ex[:], r.gap[:], ACT.Exp).then_inc(exp_ready, 1)
            if conv_out is not None:
                for b in range(B):
                    act.wait_ge(stored[b], 16 * (GROUPS // B))

        @block.gpsimd
        def _(pool):
            if layer == 0:
                nc.gpsimd.memset(r.ones[:], 1.0).then_inc(init, 1)
                nc.gpsimd.memset(r.zeros[:], 0.0).then_inc(init, 1)
                pool.wait_ge(init, 2)

            def step(it, b, first):
                pool.wait_ge(slot_ready, B * it + b + 1)
                pool.sem_inc(pool_beat, 1)
                for t in range(GT):
                    for k in range(2):
                        c = 2 * t + k
                        nc.gpsimd.indirect_dma_start(xs, bass.IndirectOffsetOnAxis(ap=slot[:, b, c:c + 1], axis=0),
                                                     xn[:, b, t, :], None).then_inc(scattered[b], 16)
            groups(pool, step)
            pool.wait_ge(tail_ready, 1)
            for e in range(EXPERTS):
                nc.gpsimd.indirect_dma_start(xs, bass.IndirectOffsetOnAxis(ap=tail_i[:, e:e + 1], axis=0),
                                             r.zeros[:], None).then_inc(tails, 16)
            for b in range(B):
                pool.wait_ge(scattered[b], 16 * 2 * GT * (GROUPS // B))
            pool.wait_ge(tails, 16 * EXPERTS)

        @block.tensor
        def _(pe):
            pe.wait_ge(consts_in, 16 if layer else 112)
            if layer == 0:
                pe.wait_ge(init, 2)

            def turn(it, b, first):
                pe.wait_ge(xn_ready, B * it + b + 1)
                for t in range(GT):
                    ins = nc.tensor.transpose(ps_t[b][:, t * P:(t + 1) * P], xn[:, b, t, :], r.ident[:])
                ins.then_inc(turned, 1)

            def logits(it, b, first):
                pe.wait_ge(xnt_ready, B * it + b + 1)
                for t in range(GT):
                    ins = nc.tensor.matmul(ps_l[b][:, t * EXPERTS:(t + 1) * EXPERTS], xnt[:, b, t * P:(t + 1) * P], r.wg[:],
                                           start=True, stop=True)
                ins.then_inc(logits_ready, 1)

            def ranks(it, b):
                pe.wait_ge(picked_ready, B * it + b + 1)
                nc.tensor.matmul(ps_rank[:, 0:GT * EXPERTS], r.before[:], picked[:, b].rearrange("p t e -> p (t e)"),
                                 start=True, stop=False)
                for t in range(GT - 1):
                    n = GT - 1 - t
                    nc.tensor.matmul(ps_rank[:, (t + 1) * EXPERTS:GT * EXPERTS], r.ones[:],
                                     picked[:, b, t, :].unsqueeze(1).to_broadcast([P, n, EXPERTS]), start=False, stop=False)
                nc.tensor.matmul(ps_rank[:, 0:GT * EXPERTS], r.ones[:],
                                 before_group[:, b, :].unsqueeze(1).to_broadcast([P, GT, EXPERTS]),
                                 start=False, stop=True).then_inc(rank_ready, 1)

            def step(it, b, first):
                if not (first and b == 0):
                    ranks(it if b else it - 1, (b - 1) % B)
                turn(it, b, first)
                logits(it, b, first)
            groups(pe, step)
            ranks(GROUPS // B - 1, B - 1)
            pe.wait_ge(total_ready, 1)
            nc.tensor.matmul(ps_rank[:, 0:EXPERTS], r.ones[:], before_group[:, 0, :], start=True, stop=True).then_inc(counted, 1)

        @block.vector
        def _(dve):
            dve.wait_ge(consts_in, 16 if layer else 112)
            nc.vector.memset(before_group[:, 0, :], 0.0).then_inc(chain, 1)
            dve.wait_ge(chain, 1)
            NORM, PICK, SLOT = (3 if conv_out is None else 4), 6, 3
            PER = NORM + PICK + SLOT

            def normalise(it, b, first, ch):
                if not first:
                    dve.wait_ge(scattered[b], 2 * GT * 16 * it)
                dve.wait_ge(x_in[b], 16 * LOADS * (it + 1))
                if conv_out is not None:
                    ch.after(nc.vector.tensor_tensor(xt[:, b], xt[:, b], zt[:, b], ALU.add))
                    dve.sem_inc(xsum_ready, 1)
                for t in range(GT):
                    ins = nc.vector.bn_stats(stats[:, t, :], xt[:, b, t, :])
                ch.after(ins, beat)
                for t in range(GT):
                    ins = nc.vector.bn_aggr(mv[:, t, :], stats[:, t, :])
                ch.after(ins)
                nc.vector.tensor_scalar(rstd[:], mv[:, :, 1], 1e-5, None, ALU.add).then_inc(var_ready, 1)
                dve.wait_ge(std_ready, B * it + b + 1)
                ch.after(nc.vector.reciprocal(rstd[:], rstd[:]))
                for t in range(GT):
                    ins = nc.vector.tensor_scalar(xn[:, b, t, :], xt[:, b, t, :], mv[:, t, 0:1], rstd[:, t:t + 1],
                                                  ALU.subtract, ALU.mult)
                ins.then_inc(xn_ready, 1)

            def pick(it, b, ch):
                g = B * it + b
                dve.wait_ge(logits_ready, g + 1)
                dve.sem_inc(beat, 1)
                for t in range(GT):
                    ins = nc.vector.max(top[:, t, :], ps_l[b][:, t * EXPERTS:(t + 1) * EXPERTS])
                ch.after(ins, beat)
                for t in range(GT):
                    ins = nc.vector.max_index(top_at[:, t, :], top[:, t, :], ps_l[b][:, t * EXPERTS:(t + 1) * EXPERTS])
                ch.after(ins)
                nc.vector.tensor_tensor(r.gap[:, bass.ds(g * GT, GT)], top[:, :, 1], top[:, :, 0], ALU.subtract)
                ch.after(nc.vector.tensor_copy(at[:].rearrange("p (t k) -> p t k", k=2), top_at[:, :, 0:2]))
                ch.after(nc.vector.tensor_tensor(onehot[:, b].rearrange("p t k e -> p (t k) e"), r.iota8[:],
                                                 at[:].unsqueeze(2).to_broadcast([P, 2 * GT, EXPERTS]), ALU.is_equal))
                ch.after(nc.vector.tensor_tensor(picked[:, b], onehot[:, b, :, 0, :], onehot[:, b, :, 1, :], ALU.add))
                dve.sem_inc(picked_ready, 1)
                ch.after(nc.vector.tensor_reduce(group_sum[:], picked[:, b].rearrange("p t e -> p e t"), AX.X, ALU.add))
                nc.vector.tensor_tensor(before_group[:, (b + 1) % B, :], before_group[:, b, :], group_sum[:], ALU.add)

            def place(it, b, ch):
                g = B * it + b
                dve.wait_ge(rank_ready, g + 1)
                ch.after(nc.vector.tensor_tensor(rank[:], ps_rank[:, 0:GT * EXPERTS], r.region[:], ALU.add))
                ch.after(nc.vector.tensor_tensor(
                    prod[:], onehot[:, b], rank[:].rearrange("p (t e) -> p t e", e=EXPERTS).unsqueeze(2).to_broadcast(
                        [P, GT, 2, EXPERTS]), ALU.mult))
                ch.after(nc.vector.tensor_reduce(slot_f[:], prod[:].rearrange("p t k e -> p (t k) e"), AX.X, ALU.add))
                nc.vector.tensor_copy(r.slots_f[:, bass.ds(g * 2 * GT, 2 * GT)], slot_f[:])
                nc.vector.tensor_copy(slot[:, b], slot_f[:]).then_inc(slot_ready, 1)

            def step(it, b, first):
                ch = Chain(dve, chain, 1 + (B * it + b) * PER - (PICK + SLOT if not (first and b == 0) else 0))
                prev = (it if b else it - 1, (b - 1) % B)
                if not (first and b == 0):
                    pick(*prev, ch)
                normalise(it, b, first, ch)
                if not (first and b == 0):
                    place(*prev, ch)
            groups(dve, step)
            ch = Chain(dve, chain, 1 + GROUPS * PER - (PICK + SLOT))
            last = (GROUPS // B - 1, B - 1)
            pick(*last, ch)
            place(*last, ch)
            ch.after(nc.vector.memset(ex[:, 0:1], 0.0))
            dve.sem_inc(total_ready, 1)
            dve.sem_inc(gap_ready, 1)
            dve.wait_ge(counted, 1)
            ch.after(nc.vector.tensor_copy(count[:], ps_rank[:, 0:EXPERTS]))
            nc.vector.tensor_tensor(tail_i[:], count[:], r.tail[:], ALU.add).then_inc(tail_ready, 1)
            ch.after(nc.vector.tensor_scalar(nblk_i[:], count[:], float(P - 1), None, ALU.add))
            ch.after(nc.vector.tensor_scalar(nblk_i[:], nblk_i[:], 7, None, ALU.arith_shift_right))
            ch.after(nc.vector.tensor_copy(nblk[:], nblk_i[:]))
            ch.after(nc.vector.tensor_copy(upto[:, 0:1], nblk[:, 0:1]))
            for e in range(1, EXPERTS):
                ch.after(nc.vector.tensor_tensor(upto[:, e:e + 1], upto[:, e - 1:e], nblk[:, e:e + 1], ALU.add))
            wide = lambda v: v[0:1, :].unsqueeze(1).to_broadcast([1, TABLE, EXPERTS])
            ch.after(nc.vector.tensor_tensor(passed[:], r.block_no[:], wide(upto), ALU.is_ge))
            ch.after(nc.vector.tensor_tensor(passed_n[:], passed[:], wide(nblk), ALU.mult))
            ch.after(nc.vector.tensor_reduce(t_e[:], passed[:], AX.X, ALU.add))
            ch.after(nc.vector.tensor_reduce(t_prev[:], passed_n[:], AX.X, ALU.add))
            ch.after(nc.vector.tensor_scalar(t_m[:], t_e[:], float(EXPERTS), None, ALU.is_lt))
            ch.after(nc.vector.tensor_tensor(t_j[:], r.block_no[:, :, 0], t_prev[:], ALU.subtract))
            ch.after(nc.vector.scalar_tensor_tensor(t_j[:], t_j[:], float(P), t_m[:], ALU.mult, ALU.mult))
            ch.after(nc.vector.tensor_scalar(t_e[:], t_e[:], float(EXPERTS - 1), None, ALU.min))
            ch.after(nc.vector.tensor_scalar(closer[:], nblk[:], float(P), float(-REGION), ALU.mult, ALU.add))
            ch.after(nc.vector.tensor_copy(out_slot[:], r.slots_f[:]))
            for e in range(1, EXPERTS):
                ch.after(nc.vector.tensor_scalar(moved[:], r.slots_f[:], float(e * REGION), closer[:, e - 1:e], ALU.is_ge, ALU.mult))
                ch.after(nc.vector.tensor_tensor(out_slot[:], out_slot[:], moved[:], ALU.add))
            nc.vector.tensor_copy(r.slots[:], out_slot[:])
            ch.after(nc.vector.scalar_tensor_tensor(t_f[:], t_e[:], float(REGION), t_j[:], ALU.mult, ALU.add))
            nc.vector.tensor_copy(r.table[:, 0, :], t_f[:])
            ch.after(nc.vector.tensor_scalar(r.table[:, 1, :], t_e[:], float(FF), None, ALU.mult))
            dve.wait_ge(w_split, 1)
            nc.vector.tensor_tensor(wt.w1l[:], wt.w1f[:], wt.w1h[:].bitcast(F32), ALU.subtract)
            dve.wait_ge(exp_ready, 1)
            ch.after(nc.vector.tensor_scalar(r.weight[:, :, 1], ex[:], 1.0, None, ALU.add))
            ch.after(nc.vector.reciprocal(r.weight[:, :, 0], r.weight[:, :, 1]))
            ch.after(nc.vector.tensor_tensor(r.weight[:, :, 1], ex[:], r.weight[:, :, 0], ALU.mult))


def expert_phase(nc, r, wt, layer, xs, ys):
    chunks = FF // P if layer == 0 else FF // P // 2
    HID = chunks * P
    with ExitStack() as ctx:
        sb = lambda n, s, d=F32: ctx.enter_context(nc.sbuf_tensor(f"e{layer}_{n}", s, d))
        sem = ctx.enter_context(stage_semaphores(nc, f"e{layer}_"))
        ps = lambda n: [ctx.enter_context(nc.psum_tensor(f"e{layer}_ps_{n}{i}", [P, 512], F32)) for i in range(2)]
        U, AHEAD = 8, 6
        xg = sb("xg", [P, U, P])
        xh, xl = sb("xh", [P, 2, P], F32R), sb("xl", [P, 2, P], F32R)
        gate = sb("gate", [P, 2, FF // 2]) if layer else None
        h, ht, y = sb("h", [P, 2, HID]), sb("ht", [P, 2, HID]), sb("y", [P, U, P])
        ps_x, ps_h, ps_ht, ps_y = ps("x"), ps("h"), ps("ht"), ps("y")
        x_in = [sem(f"x_in{s}") for s in range(U)]
        stored = [sem(f"stored{s}") for s in range(U)]
        x_turned, x_split, h_ready, gated, hid_ready, h_turned, ht_ready, y_done, y_ready, hi_done = (
            sem(n) for n in ("x_turned", "x_split", "h_ready", "gated", "hid_ready", "h_turned", "ht_ready", "y_done",
                             "y_ready", "hi_done"))
        block = ctx.enter_context(nc.Block())
        STEPS = BLOCKS // U

        def steps(eng, step):
            for s in range(U):
                step(0, s, True)
            with eng.Fori(1, STEPS) as it:
                for s in range(U):
                    step(it, s, False)

        @block.sync
        def _(sp):
            row = lambda b: sp.value_load(r.table[0:1, 0, bass.ds(b, 1)], min_val=0, max_val=EXPERTS * REGION - P)

            def load(b, slot, again):
                if again:
                    sp.wait_ge(x_turned, b - U + 1)
                sp.dma_start(xg[:, slot, :], xs[bass.ds(row(b), P), :]).then_inc(x_in[slot], 16)

            for s in range(AHEAD):
                load(s, s, False)

            def step(it, s, first):
                b = U * it + s
                load(b + AHEAD, (s + AHEAD) % U, not first or s + AHEAD >= U)
                sp.wait_ge(y_ready, b + 1)
                sp.dma_start(ys[bass.ds(b * P, P), :], y[:, s, :]).then_inc(stored[s], 16)
            steps(sp, step)
            for s in range(U):
                sp.wait_ge(stored[s], 16 * (STEPS + (1 if s == U - 1 else 0)))
                sp.wait_ge(x_in[s], 16 * (STEPS + (1 if s < AHEAD else 0)))

        @block.tensor
        def _(pe):
            def weights_of(b, n):
                return nc.values_load_multi_w_load_instructions(
                    r.table[0:1, 1, bass.ds(b, n)], engines=[mybir.EngineType.PE], min_val=0, max_val=(EXPERTS - 1) * FF)[1]

            def turn_x(b, s, turn_no, early):
                pe.wait_ge(x_in[s % U], 16 * (turn_no + 1))
                if not early:
                    pe.wait_ge(x_split, b - 1)
                nc.tensor.transpose(ps_x[s % 2][:, 0:P], xg[:, s % U, :], r.ident[:]).then_inc(x_turned, 1)

            def first_product(b, s, w, early):
                pe.wait_ge(x_split, b + 1)
                if not early:
                    pe.wait_ge(hid_ready, b - 1)
                i = s % 2
                nc.tensor.matmul(ps_h[i][:], xl[:, i, :], wt.w1h[:, bass.ds(w, FF)], start=True, stop=False)
                nc.tensor.matmul(ps_h[i][:], xh[:, i, :], wt.w1l[:, bass.ds(w, FF)], start=False, stop=False)
                nc.tensor.matmul(ps_h[i][:], xh[:, i, :], wt.w1h[:, bass.ds(w, FF)], start=False, stop=True
                                 ).then_inc(h_ready, 1)

            def turn_h(b, s, early):
                pe.wait_ge(hid_ready, b + 1)
                if not early:
                    pe.wait_ge(ht_ready, b - 1)
                for c in range(chunks):
                    ins = nc.tensor.transpose(ps_ht[s % 2][:, c * P:(c + 1) * P], h[:, s % 2, c * P:(c + 1) * P], r.ident[:])
                ins.then_inc(h_turned, 1)

            def second_product(b, s, w, early):
                pe.wait_ge(ht_ready, b + 1)
                if not early:
                    pe.wait_ge(y_ready, b - 1)
                for c in range(chunks):
                    ins = nc.tensor.matmul(ps_y[s % 2][:, 0:P], ht[:, s % 2, c * P:(c + 1) * P],
                                           wt.w2[:, bass.ds(w + c * P, P)], start=c == 0, stop=c == chunks - 1)
                ins.then_inc(y_done, 1)

            w = {}
            w[1], w[2] = weights_of(0, 2)
            for s in range(2):
                turn_x(s, s, 0, True)
            for s in range(2):
                first_product(s, s, w[s + 1], True)
            turn_x(2, 2, 0, False)

            def step(it, s, first):
                b = U * it + s
                turn_h(b, s, first and s < 2)
                turn_x(b + 3, s + 3, it + (1 if s + 3 >= U else 0), False)
                if s == 0 and not first:
                    w.update(enumerate(weights_of(b - 1, 3)))
                if not (first and s == 0):
                    second_product(b - 1, s - 1, w[s], first and s < 3)
                w[s + 3] = weights_of(b + 2, 1)[0]
                first_product(b + 2, s + 2, w[s + 3], False)
            steps(pe, step)
            second_product(BLOCKS - 1, U - 1, w[U], False)

        @block.scalar
        def _(act):
            def activate(b, s, early):
                act.wait_ge(h_ready, b + 1)
                i = s % 2
                if layer:
                    if not early:
                        act.wait_ge(hid_ready, b - 1)
                    nc.scalar.activation(gate[:, i, :], ps_h[i][:, 0:HID], ACT.Silu).then_inc(gated, 1)
                else:
                    if not early:
                        act.wait_ge(h_turned, b - 1)
                    nc.scalar.activation(h[:, i, :], ps_h[i][:], ACT.Silu).then_inc(hid_ready, 1)

            def answer(b, s, turn_no, early):
                act.wait_ge(y_done, b + 1)
                if not early:
                    act.wait_ge(stored[s % U], 16 * turn_no)
                nc.scalar.activation(y[:, s % U, :], ps_y[s % 2][:, 0:P], ACT.Copy).then_inc(y_ready, 1)

            act.sem_inc(stored[U - 1], 16)
            activate(0, 0, True)
            activate(1, 1, True)

            def step(it, s, first):
                b = U * it + s
                if not (first and s == 0):
                    answer(b - 1, s - 1, it, first)
                activate(b + 2, s + 2, False)
            steps(act, step)
            answer(BLOCKS - 1, U - 1, STEPS, False)

        @block.vector
        def _(dve):
            def split(b, s, early):
                dve.wait_ge(x_turned, b + 1)
                if not early:
                    dve.wait_ge(h_ready, b - 1)
                i = s % 2
                nc.vector.tensor_copy(xh[:, i, :], ps_x[i][:, 0:P]).then_inc(hi_done, 1)
                dve.wait_ge(hi_done, b + 1)
                nc.vector.tensor_tensor(xl[:, i, :], ps_x[i][:, 0:P], xh[:, i, :].bitcast(F32), ALU.subtract
                                        ).then_inc(x_split, 1)

            def gate_product(b, s, early):
                dve.wait_ge(gated, b + 1)
                if not early:
                    dve.wait_ge(h_turned, b - 1)
                i = s % 2
                nc.vector.tensor_tensor(h[:, i, :], gate[:, i, :], ps_h[i][:, HID:2 * HID], ALU.mult
                                        ).then_inc(hid_ready, 1)

            split(0, 0, True)
            split(1, 1, True)
            split(2, 2, False)
            if layer:
                gate_product(0, 0, True)
                gate_product(1, 1, True)

            def step(it, s, first):
                b = U * it + s
                dve.wait_ge(h_turned, b + 1)
                if not (first and s < 2):
                    dve.wait_ge(y_done, b - 1)
                nc.vector.tensor_copy(ht[:, s % 2, :], ps_ht[s % 2][:, 0:HID]).then_inc(ht_ready, 1)
                split(b + 3, s + 3, False)
                if layer:
                    gate_product(b + 2, s + 2, False)
            steps(dve, step)


def combine_phase(nc, r, layer, ys, src, dst, normed=None):
    with ExitStack() as ctx:
        sb = lambda n, s, d=F32: ctx.enter_context(nc.sbuf_tensor(f"m{layer}_{n}", s, d))
        sem = ctx.enter_context(stage_semaphores(nc, f"m{layer}_"))
        B = 3
        xt, xn = sb("xt", [P, B, GT, P]), sb("xn", [P, B, GT, P])
        yg = sb("yg", [P, B, GT, 2, P])
        slot = sb("slot", [P, B, 2 * GT], I32)
        stats, mv, rstd = sb("stats", [P, GT, 6]), sb("mv", [P, GT, 2]), sb("rstd", [P, GT])
        x_in, y_in, stored = ([sem(f"{n}{b}") for b in range(B)] for n in ("x_in", "y_in", "stored"))
        beat, pool_beat, chain, var_ready, std_ready, x_ready, xn_ready, slot_ready = (
            sem(n) for n in ("beat", "pool_beat", "chain", "var", "std", "x_ready", "xn_ready", "slot_ready"))
        block = ctx.enter_context(nc.Block())
        rows = lambda dram, g: dram[bass.ds(g * GT * P, GT * P), :].rearrange("(t p) c -> p t c", p=P)
        STORES = 1 if normed is None else 2

        def groups(eng, step):
            for b in range(B):
                step(0, b, True)
            with eng.Fori(1, GROUPS // B) as it:
                for b in range(B):
                    step(it, b, False)

        @block.sync
        def _(sp):
            def load(it, b, first):
                if not first:
                    sp.wait_ge(stored[b], 16 * STORES * it)
                sp.dma_start(xt[:, b], rows(src, B * it + b)).then_inc(x_in[b], 16)
            groups(sp, load)

        @block.gpsimd
        def _(pool):
            def gather(it, b, first):
                if not first:
                    pool.wait_ge(x_ready, B * it + b - B + 1)
                nc.gpsimd.tensor_copy(slot[:, b], r.slots[:, bass.ds(2 * GT * (B * it + b), 2 * GT)]).then_inc(slot_ready, 1)
                pool.wait_ge(slot_ready, B * it + b + 1)
                pool.sem_inc(pool_beat, 1)
                for t in range(GT):
                    for k in range(2):
                        c = 2 * t + k
                        nc.gpsimd.indirect_dma_start(yg[:, b, t, k, :], None, ys,
                                                     bass.IndirectOffsetOnAxis(ap=slot[:, b, c:c + 1], axis=0)
                                                     ).then_inc(y_in[b], 16)
            groups(pool, gather)

        @block.scalar
        def _(act):
            def step(it, b, first):
                if normed is not None:
                    act.wait_ge(var_ready, B * it + b + 1)
                    nc.scalar.activation(rstd[:], rstd[:], ACT.Sqrt).then_inc(std_ready, 1)
                act.wait_ge(x_ready, B * it + b + 1)
                act.dma_start(rows(dst, B * it + b), xt[:, b]).then_inc(stored[b], 16)
                if normed is not None:
                    act.wait_ge(xn_ready, B * it + b + 1)
                    act.dma_start(rows(normed, B * it + b), xn[:, b]).then_inc(stored[b], 16)
            groups(act, step)
            for b in range(B):
                act.wait_ge(stored[b], 16 * STORES * (GROUPS // B))

        @block.vector
        def _(dve):
            PER = 1 if normed is None else 5

            def step(it, b, first):
                g = B * it + b
                ch = Chain(dve, chain, g * PER)
                dve.wait_ge(x_in[b], 16 * (it + 1))
                dve.wait_ge(y_in[b], 16 * 2 * GT * (it + 1))
                for k in range(2):
                    for t in range(GT):
                        ins = nc.vector.scalar_tensor_tensor(xt[:, b, t, :], yg[:, b, t, k, :],
                                                             r.weight[:, bass.ds(GT * g + t, 1), k], xt[:, b, t, :],
                                                             ALU.mult, ALU.add)
                    if k == 0:
                        ch.after(ins)
                ins.then_inc(x_ready, 1)
                if normed is None:
                    return
                dve.wait_ge(x_ready, g + 1)
                for t in range(GT):
                    ins = nc.vector.bn_stats(stats[:, t, :], xt[:, b, t, :])
                ch.after(ins, beat)
                for t in range(GT):
                    ins = nc.vector.bn_aggr(mv[:, t, :], stats[:, t, :])
                ch.after(ins)
                nc.vector.tensor_scalar(rstd[:], mv[:, :, 1], 1e-6, None, ALU.add).then_inc(var_ready, 1)
                dve.wait_ge(std_ready, g + 1)
                ch.after(nc.vector.reciprocal(rstd[:], rstd[:]))
                if not first:
                    dve.wait_ge(stored[b], 16 * STORES * it)
                for t in range(GT):
                    ins = nc.vector.tensor_scalar(xn[:, b, t, :], xt[:, b, t, :], mv[:, t, 0:1], rstd[:, t:t + 1],
                                                  ALU.subtract, ALU.mult)
                ch.after(ins)
                dve.sem_inc(xn_ready, 1)
            groups(dve, step)


def conv1_phase(nc, io, xn_d, z_d):
    with ExitStack() as ctx:
        sb = lambda n, s, d=F32: ctx.enter_context(nc.sbuf_tensor(f"c1_{n}", s, d))
        sem = ctx.enter_context(stage_semaphores(nc, f"c1_"))
        fa, fb = sb("fa", [P, N_UP * PPX + N_DOWN * TPX]), sb("fb", [P, N_UP * PPX + N_DOWN * TPX])
        gh, gl = sb("gh", [P, N_UP * PPX + N_DOWN * TPX], F32R), sb("gl", [P, N_UP * PPX + N_DOWN * TPX], F32R)
        xf = sb("xf", [P, 2, QT, NC])
        xh, xl = sb("xh", [P, 2, QT, NC], F32R), sb("xl", [P, 2, QT, NC], F32R)
        a, c = sb("a", [P, 2, NC]), sb("c", [P, 2, NC])
        yh, yl = sb("yh", [P, 2, NC], F32R), sb("yl", [P, 2, NC], F32R)
        zs = sb("zs", [P, 2, NC])
        ps_y = [ctx.enter_context(nc.psum_tensor(f"c1_py{i}", [P, 512], F32)) for i in range(2)]
        ps_z = [ctx.enter_context(nc.psum_tensor(f"c1_pz{i}", [P, 512], F32)) for i in range(2)]
        factors_in, xf_clear, g_ready, gh_ready, gl_ready = (sem(n) for n in ("factors", "clear", "g", "gh", "gl"))
        bias_in, x_in = sem("bias_in"), [sem(f"x_in{i}") for i in range(2)]
        xh_ready, xl_ready, y_raw, y_act, y_leaky, y_clip, y_hi, y_split, down_done = (
            sem(n) for n in ("xh", "xl", "y_raw", "y_act", "y_leaky", "y_clip", "y_hi", "y_split", "down_done"))
        z_copied, zs_free, z_stored = (sem(n) for n in ("z_copied", "zs_free", "z_stored"))
        CREDIT = 2
        PAIRS2 = 2 * PAIRS
        LAG = 3
        UPW = N_UP * PPX
        up_w = lambda m: slice(m * PPX, (m + 1) * PPX)
        down_w = lambda m, n: slice(UPW + m * TPX, UPW + m * TPX + n)
        tile_rows = lambda q: (ROWS if q < QT - 1 else SIDE - ROWS * (QT - 1)) * SIDE
        last_pair = lambda q: min(ROWS * q + 2 * ROWS - 1, PAIRS - 1)
        done_at = {i * PAIRS + last_pair(q): i * QT + q for i in range(2) for q in range(QT)}
        block = ctx.enter_context(nc.Block())

        def dram_tile(d, ig, q):
            v = d.rearrange("(n p) c -> p n c", p=PIXELS)
            return v[q * TPX:q * TPX + tile_rows(q), bass.ds(ig * IG, IG), :]

        @block.sync
        def _(sp):
            sp.sem_inc(zs_free, CREDIT)
            sp.dma_start(fa[:, 0:UPW], io["up_a"].rearrange("p m k -> p (m k)")).then_inc(factors_in, 16)
            sp.dma_start(fb[:, 0:UPW], io["up_b"].rearrange("p m k -> p (m k)")).then_inc(factors_in, 16)
            sp.dma_start(fa[:, UPW:], io["down_a"].rearrange("p m k -> p (m k)")).then_inc(factors_in, 16)
            sp.dma_start(fb[:, UPW:], io["down_b"].rearrange("p m k -> p (m k)")).then_inc(factors_in, 16)
            sp.wait_ge(xf_clear, 1)
            for i in range(2):
                sp.dma_start(xf[TPX:TPX + 1, i], io["bias1"]).then_inc(bias_in, 16)
            with sp.Fori(0, IMAGE_GROUPS // 2) as it:
                for i in range(2):
                    sp.wait_ge(xl_ready, 2 * it + i + 1)
                    for q in range(QT):
                        sp.dma_start(xf[0:tile_rows(q), i, q, :].rearrange("p (n c) -> p n c", c=P),
                                     dram_tile(xn_d, 2 * it + i, q)).then_inc(x_in[i], 16)
                for m in range(2 * QT):
                    q = m % QT
                    sp.wait_ge(z_copied, CREDIT + 2 * QT * it + m + 1)
                    sp.dma_start(dram_tile(z_d, 2 * it + m // QT, q),
                                 zs[0:tile_rows(q), m % 2, :].rearrange("p (n c) -> p n c", c=P)).then_inc(z_stored, 16)
                    sp.wait_ge(z_stored, 16 * (2 * QT * it + m + 1))
                    sp.sem_inc(zs_free, 1)

        @block.gpsimd
        def _(pool):
            nc.gpsimd.memset(xf[:], 0.0).then_inc(xf_clear, 1)

        @block.tensor
        def _(pe):
            def three(out, wcols, k, mv_h, mv_l, start, stop):
                ins = None
                for n, (w, v) in enumerate(((gl, mv_h), (gh, mv_l), (gh, mv_h))):
                    ins = nc.tensor.matmul(out, w[0:k, wcols], v, start=start and n == 0, stop=stop and n == 2)
                return ins

            def up(it, n):
                i, p = divmod(n, PAIRS)
                if p == 0:
                    pe.wait_ge(xl_ready, CREDIT + 2 * it + i + 1)
                pe.wait_ge(y_act, PAIRS2 * it + n + 1)
                t, rho = divmod(p, ROWS)
                parts = []
                if t >= 1:
                    parts.append((2 * ROWS + rho, TPX + 1, t - 1) if t == QT else (rho, TPX, t - 1))
                if t < QT:
                    parts.append((ROWS + rho, TPX + 1, t))
                for j, (m, k, q) in enumerate(parts):
                    ins = three(ps_y[n % 2][0:PPX, :], up_w(m), k, xh[0:k, i, q, :], xl[0:k, i, q, :],
                                j == 0, j == len(parts) - 1)
                ins.then_inc(y_raw, 1)

            def down(it, n):
                i, p = divmod(n, PAIRS)
                pe.wait_ge(y_split, CREDIT + PAIRS2 * it + n + 1)
                t, rho = divmod(p, ROWS)
                for q, m in ((t - 1, ROWS + rho), (t, rho)):
                    if not 0 <= q < QT:
                        continue
                    z, rows = i * QT + q, tile_rows(q)
                    if p == ROWS * q:
                        pe.wait_ge(z_copied, 2 * QT * it + z + 1)
                    ins = three(ps_z[z % 2][0:rows, :], down_w(m, rows), PPX, yh[0:PPX, n % 2, :], yl[0:PPX, n % 2, :],
                                p == ROWS * q, p == last_pair(q))
                ins.then_inc(down_done, 1)

            pe.sem_inc(down_done, CREDIT)
            pe.wait_ge(gl_ready, 1)
            with pe.Fori(0, IMAGE_GROUPS // 2) as it:
                for n in range(PAIRS2 + LAG):
                    if n < PAIRS2:
                        up(it, n)
                    if n >= LAG:
                        down(it, n - LAG)

        @block.scalar
        def _(act):
            act.sem_inc(y_act, CREDIT)
            act.sem_inc(z_copied, CREDIT)
            act.wait_ge(g_ready, 1)
            nc.scalar.activation(gh[:], fa[:], ACT.Copy).then_inc(gh_ready, 1)

            def split_x(it, i):
                if i == 0:
                    act.wait_ge(bias_in, 32)
                act.wait_ge(x_in[i], 16 * QT * (it + 1))
                nc.scalar.activation(xh[:, i], xf[:, i], ACT.Copy).then_inc(xh_ready, 1)

            def gain(it, n):
                act.wait_ge(y_raw, PAIRS2 * it + n + 1)
                act.wait_ge(y_clip, PAIRS2 * it + n + 1)
                nc.scalar.activation(a[0:PPX, n % 2, :], ps_y[n % 2][0:PPX, :], ACT.Copy, scale=float(np.sqrt(2.0))
                                     ).then_inc(y_act, 1)

            def high(it, n):
                act.wait_ge(y_clip, CREDIT + PAIRS2 * it + n + 1)
                act.wait_ge(down_done, PAIRS2 * it + n + 1)
                nc.scalar.activation(yh[0:PPX, n % 2, :], c[0:PPX, n % 2, :], ACT.Copy).then_inc(y_hi, 1)

            def copy_z(it, z, n):
                act.wait_ge(down_done, CREDIT + PAIRS2 * it + n + 1)
                act.wait_ge(zs_free, 2 * QT * it + z + 1)
                rows = tile_rows(z % QT)
                nc.scalar.activation(zs[0:rows, z % 2, :], ps_z[z % 2][0:rows, :], ACT.Copy).then_inc(z_copied, 1)

            with act.Fori(0, IMAGE_GROUPS // 2) as it:
                split_x(it, 0)
                for n in range(PAIRS2 + LAG):
                    if n < PAIRS2:
                        gain(it, n)
                    if 1 <= n <= PAIRS2:
                        high(it, n - 1)
                    if n == 4:
                        split_x(it, 1)
                    if n - LAG in done_at:
                        copy_z(it, done_at[n - LAG], n - LAG)

        @block.vector
        def _(dve):
            dve.sem_inc(xl_ready, CREDIT)
            dve.sem_inc(y_split, CREDIT)
            dve.wait_ge(factors_in, 64)
            nc.vector.scalar_tensor_tensor(fa[:, 0:UPW], fa[:, 0:UPW], 4.0, fb[:, 0:UPW], ALU.mult, ALU.mult)
            nc.vector.tensor_tensor(fa[:, UPW:], fa[:, UPW:], fb[:, UPW:], ALU.mult).then_inc(g_ready, 1)
            dve.wait_ge(gh_ready, 1)
            nc.vector.tensor_tensor(gl[:], fa[:], gh[:].bitcast(F32), ALU.subtract).then_inc(gl_ready, 1)

            def split_x(it, i):
                dve.wait_ge(xh_ready, 2 * it + i + 1)
                nc.vector.tensor_tensor(xl[:, i], xf[:, i], xh[:, i].bitcast(F32), ALU.subtract).then_inc(xl_ready, 1)

            def leaky(it, n):
                k = n % 2
                dve.wait_ge(y_act, CREDIT + PAIRS2 * it + n + 1)
                dve.wait_ge(y_split, PAIRS2 * it + n + 1)
                nc.vector.scalar_tensor_tensor(c[0:PPX, k, :], a[0:PPX, k, :], 0.2, a[0:PPX, k, :], ALU.mult, ALU.max
                                               ).then_inc(y_leaky, 1)
                dve.wait_ge(y_leaky, PAIRS2 * it + n + 1)
                nc.vector.tensor_scalar(c[0:PPX, k, :], c[0:PPX, k, :], 256.0, -256.0, ALU.min, ALU.max).then_inc(y_clip, 1)

            def low(it, n):
                k = n % 2
                dve.wait_ge(y_hi, PAIRS2 * it + n + 1)
                nc.vector.tensor_tensor(yl[0:PPX, k, :], c[0:PPX, k, :], yh[0:PPX, k, :].bitcast(F32), ALU.subtract
                                        ).then_inc(y_split, 1)

            dve.sem_inc(y_clip, CREDIT)
            with dve.Fori(0, IMAGE_GROUPS // 2) as it:
                split_x(it, 0)
                for n in range(PAIRS2 + 1):
                    if n < PAIRS2:
                        leaky(it, n)
                    if n == 4:
                        split_x(it, 1)
                    if n >= 1:
                        low(it, n - 1)


def host_layouts(a):
    f32 = np.float32
    x = np.asarray(a["x"])
    io = {}
    xh = np.zeros((CGS, RPAD, IMAGES, SIDE, CIN), f32)
    xh[:, :SIDE] = x.reshape(IMAGES, CGS, CIN, SIDE, SIDE).transpose(1, 3, 0, 4, 2)
    io["xh"] = xh.reshape(P, NW, CIN)
    c = np.arange(P).reshape(P, 1, 1)
    kh, kw = np.arange(TAPS).reshape(1, TAPS, 1), np.arange(TAPS).reshape(1, 1, TAPS)
    idx = (c * 1337 + kh * 7919 + kw * 2971 + 3 * 104729) % 1024
    taps = np.asarray(a["L0_conv_codebook"])[idx].reshape(CGS, CIN, TAPS, TAPS)
    w0 = np.zeros((CIN, CGS, RPAD, TAPS, CGS, RPAD), f32)
    for ho in range(SIDE):
        for hi in range(max(0, ho - HALO), min(SIDE, ho + HALO + 1)):
            for g in range(CGS):
                w0[:, g, hi, :, g, ho] = taps[g, :, hi - ho + HALO, :]
    io["w0"] = w0.reshape(CIN, P, KLEN)
    b = np.asarray(a["L0_conv_bias"]).reshape(CGS, 1, CIN)
    io["bias0"] = np.ascontiguousarray(np.broadcast_to(b, (CGS, RPAD, CIN))).reshape(P, CIN)
    row = np.arange(P) % RPAD
    io["mean_w"] = ((row[:, None] == row[None, :]) & (row < SIDE)[:, None] & (row < SIDE)[None, :]).astype(f32) / f32(P)
    col = np.arange(NW) % SIDE
    io["check"] = np.stack([1.0 - 2.0 * ((row[:, None] + col) % 2), 1.0 - 2.0 * (col % 2) + 0 * row[:, None]], 1).astype(f32)
    sgn = 1.0 - 2.0 * (row % 2)
    io["osign"] = np.stack([-sgn, sgn], 1).astype(f32)
    io["wg0"] = np.asarray(a["L0_ffn_Wg"])
    io["wg1"] = np.asarray(a["L1_ffn_router_w"])
    io["w1_0"] = np.asarray(a["L0_ffn_W1"]).transpose(1, 0, 2)
    io["w2_0"] = np.asarray(a["L0_ffn_W2"]).reshape(EXPERTS, 4, P, P).transpose(2, 0, 1, 3)
    io["w1_1"] = np.concatenate([np.asarray(a["L1_ffn_w1"]), np.asarray(a["L1_ffn_w3"])], 2).transpose(1, 0, 2)
    io["w2_1"] = np.asarray(a["L1_ffn_w2"]).reshape(EXPERTS, 2, P, P).transpose(2, 0, 1, 3)
    p = np.arange(P)
    io["ident"] = np.eye(P, dtype=f32)
    io["before"] = (p[:, None] < p[None, :]).astype(f32)
    io["iota8"] = np.broadcast_to(np.arange(EXPERTS, dtype=f32), (P, GT, 2, EXPERTS)).reshape(P, GT * 2 * EXPERTS)
    io["region"] = np.broadcast_to(np.arange(EXPERTS, dtype=f32) * REGION, (P, GT, EXPERTS)).reshape(P, GT * EXPERTS)
    io["tail"] = (np.arange(EXPERTS, dtype=f32) * REGION + p[:, None]).astype(f32)
    io["block_no"] = np.broadcast_to(np.arange(TABLE, dtype=f32)[:, None], (TABLE, EXPERTS)).reshape(1, TABLE * EXPERTS)
    fu, fd = np.asarray(a["L1_conv_up_filter"]), np.asarray(a["L1_conv_down_filter"])
    h, w = np.arange(P) // SIDE, np.arange(P) % SIDE
    e, j = np.arange(PPX) // UP, np.arange(PPX) % UP
    pix = (np.arange(P) < TPX)[:, None]
    fa, fb = np.zeros((P, N_UP, PPX), f32), np.zeros((P, N_UP, PPX), f32)
    mats = [(s, r, s == 1) for s in range(2) for r in range(ROWS)] + [(0, r, True) for r in range(4)]
    for m, (s, r, with_bias) in enumerate(mats):
        d = (ROWS if s == 0 else 0) + r - h[:, None]
        kr, kc = 2 * d + e[None, :], j[None, :] - 2 * w[:, None]
        fa[:, m] = np.where(pix & (kr >= 0) & (kr < FIR), fu[np.clip(kr, 0, FIR - 1)], 0)
        fb[:, m] = np.where(pix & (kc >= 0) & (kc < FIR), fu[np.clip(kc, 0, FIR - 1)], 0)
        if with_bias:
            fa[TPX, m], fb[TPX, m] = 1.0, 0.25
    io["up_a"], io["up_b"] = fa, fb
    e, j = np.arange(P) // UP, np.arange(P) % UP
    h, w = np.arange(TPX) // SIDE, np.arange(TPX) % SIDE
    pix = (np.arange(P) < PPX)[:, None]
    fa, fb = np.zeros((P, N_DOWN, TPX), f32), np.zeros((P, N_DOWN, TPX), f32)
    for m in range(N_DOWN):
        kr, kc = 2 * (m - h[None, :]) + e[:, None], j[:, None] - 2 * w[None, :]
        fa[:, m] = np.where(pix & (kr >= 0) & (kr < FIR), fd[np.clip(FIR - 1 - kr, 0, FIR - 1)], 0)
        fb[:, m] = np.where(pix & (kc >= 0) & (kc < FIR), fd[np.clip(FIR - 1 - kc, 0, FIR - 1)], 0)
    io["down_a"], io["down_b"] = fa, fb
    io["bias1"] = np.ascontiguousarray(np.broadcast_to(np.asarray(a["L1_conv_bias"]), (1, QT, IG, P))).reshape(1, QT, NC)
    return {k: np.ascontiguousarray(v) for k, v in io.items()}


def metaformer(nc, io, out):
    dram = lambda n, rows: nc.dram_tensor(n, (rows, P), F32).ap()
    x1, x2, x2n, z, x3 = (dram(n, TOKENS) for n in ("x1", "x2", "x2n", "z", "x3"))
    xs, ys = dram("routed", EXPERTS * REGION), dram("answers", BLOCKS * P)
    with ExitStack() as ctx:
        conv0_phase(nc, io, x1)
        r = Routing(nc, ctx)
        with ExitStack() as inner:
            wt = ExpertWeights(nc, inner, 0)
            route_phase(nc, io, r, wt, 0, xs, x1)
            expert_phase(nc, r, wt, 0, xs, ys)
        combine_phase(nc, r, 0, ys, x1, x2, x2n)
        conv1_phase(nc, io, x2n, z)
        with ExitStack() as inner:
            wt = ExpertWeights(nc, inner, 1)
            route_phase(nc, io, r, wt, 1, xs, x2, z, x3)
            expert_phase(nc, r, wt, 1, xs, ys)
        combine_phase(nc, r, 1, ys, x3, out)


def kernel(**inputs):
    import concourse.bacc as bacc
    from concourse.bass_utils import run_bass_kernel_spmd

    nc = bacc.Bacc("TRN2", target_bir_lowering=False, num_devices=1)
    arrays = {f"in_{k}": v for k, v in host_layouts(inputs).items()}
    io = {k[3:]: nc.dram_tensor(k, v.shape, mybir.dt.from_np(v.dtype), kind="ExternalInput").ap() for k, v in arrays.items()}
    out = nc.dram_tensor("out", (TOKENS, P), F32, kind="ExternalOutput").ap()
    metaformer(nc, io, out)
    got = run_bass_kernel_spmd(nc, [arrays], core_ids=[0]).results[0]["out"]
    return got.reshape(IMAGES, SIDE, SIDE, P).transpose(0, 3, 1, 2)
```

```python
from contextlib import ExitStack, contextmanager

import numpy as np

import concourse.bass as bass
from concourse import mybir

F32 = mybir.dt.float32
F32R = mybir.dt.float32r
BF16 = mybir.dt.bfloat16
I32 = mybir.dt.int32
U32 = mybir.dt.uint32
ALU = mybir.AluOpType
ACT = mybir.ActivationFunctionType
AX = mybir.AxisListType

P = 128
IMAGES, SIDE = 16, 24
PIXELS = SIDE * SIDE
TOKENS = IMAGES * PIXELS
TILES = TOKENS // P
EXPERTS = 8
FF = 512
BLOCKS = 2 * TILES + EXPERTS
TABLE = BLOCKS + 8
REGION = TOKENS + P
SPARE = TABLE - 2 * TILES
PAY = 132
DEST, WEIGHT = P, P + 1
NORM_STEPS, PICK_STEPS, PLACE_STEPS = 3, 6, 4

CGS, CIN, RPAD = 4, 32, 32
TAPS, HALO = 7, 3
WPAD = SIDE + 2 * HALO
NW = IMAGES * SIDE
KLEN = TAPS * P
WRING = 4

ROWS = 5
TPX = ROWS * SIDE
QT = 5
IG = 4
IMAGE_GROUPS = IMAGES // IG
GROUPS = IMAGE_GROUPS * QT
NC = IG * P
CHOICES = 2 * IG
ANSWERS = GROUPS * TPX * CHOICES

FIR = 12
UP = 58
PAIRS = UP // 2
PPX = 2 * UP
N_UP = 2 * ROWS + 4
N_DOWN = 2 * ROWS
GAIN = float(np.sqrt(2.0))


@contextmanager
def stage_semaphores(nc, prefix):
    taken = []

    def named(name):
        taken.append(nc.alloc_semaphore(name=prefix + name))
        return taken[-1]

    yield named
    nc.clear_and_free_semaphores(taken)
    nc.all_engine_barrier()


def pixels(q):
    return (ROWS if q < QT - 1 else SIDE - ROWS * (QT - 1)) * SIDE


def tile_of(dram, ig, q):
    v = dram.rearrange("(n p) c -> p n c", p=PIXELS)
    return v[q * TPX:q * TPX + pixels(q), bass.ds(ig * IG, IG), :]


def need(eng, sem, value, beat=None):
    if isinstance(value, int) and value <= 0:
        return
    eng.wait_ge(sem, value)
    if beat is not None:
        eng.sem_inc(beat, 1)


def last_user(n, ring, turn):
    return n - ring if n >= ring else max(m for m in range(turn) if m % ring == n) - turn


def groups(eng, step, between=None):
    for q in range(QT):
        step(0, q)
    if between is not None:
        between()
    with eng.Fori(1, IMAGE_GROUPS) as ig:
        for q in range(QT):
            step(ig, q)


def before(ig, q):
    if q:
        return ig, q - 1
    return None if isinstance(ig, int) and ig == 0 else (ig - 1, QT - 1)


class Chain:

    def __init__(self, eng, sem, base=0):
        self.eng, self.sem, self.base, self.n = eng, sem, base, 0

    def after(self, ins, beat=None):
        ins.then_inc(self.sem, 1)
        self.n += 1
        need(self.eng, self.sem, self.base + self.n, beat)


def conv0_phase(nc, io, x1d):
    with ExitStack() as ctx:
        sb = lambda n, s, d=F32: ctx.enter_context(nc.sbuf_tensor(n, s, d))
        sem = ctx.enter_context(stage_semaphores(nc, ""))
        x = sb("c0_x", [P, NW, CIN])
        pad = sb("c0_pad", [P, CIN, IMAGES, WPAD])
        sq = sb("c0_sq", [P, NW, CIN])
        part = sb("c0_part", [P, NW])
        rstd = sb("c0_rstd", [P, NW])
        wring = sb("c0_w", [P, WRING, KLEN])
        wh, wl = sb("c0_wh", [P, 2, KLEN], F32R), sb("c0_wl", [P, 2, KLEN], F32R)
        ph, pl = sb("c0_ph", [P, 2, IMAGES, WPAD], F32R), sb("c0_pl", [P, 2, IMAGES, WPAD], F32R)
        tmp = sb("c0_tmp", [P, 2, NW])
        bias = sb("c0_bias", [P, CIN])
        mean_w = sb("c0_meanw", [P, P])
        check = sb("c0_check", [P, 2, NW])
        osign = sb("c0_osign", [P, 2])
        ps_stat = [ctx.enter_context(nc.psum_tensor(f"c0_ps{i}", [P, 512], F32)) for i in range(4)]
        ps = [ctx.enter_context(nc.psum_tensor(f"c0_acc{i}", [P, 512], F32)) for i in range(4)]
        mean_w_in = sem("c0_mean_w_in")
        consts_in, x_in = sem("c0_consts_in"), [sem(f"c0_x_in{i}") for i in range(4)]
        w_in = [sem(f"c0_w_in{i}") for i in range(WRING)]
        padded, sums, mean_ready, centred = sem("c0_padded"), sem("c0_sums"), sem("c0_mean"), sem("c0_centred")
        var_summed, var_ready, std_ready = sem("c0_var_summed"), sem("c0_var_ready"), sem("c0_std_ready")
        squared, chain, rstd_ready, normed = sem("c0_squared"), sem("c0_chain"), sem("c0_rstd_ready"), sem("c0_normed")
        acc_ready, acc_free, x1_ready, stored = sem("c0_acc_ready"), sem("c0_acc_free"), sem("c0_x1_ready"), sem("c0_stored")
        w_free, high_ready, split_ready, act_beat = (sem(n) for n in ("c0_w_free", "c0_high", "c0_split", "c0_act_beat"))
        Q = NW // 4
        PER_STORE = 8
        block = ctx.enter_context(nc.Block())

        def store(eng, cg):
            eng.wait_ge(x1_ready, CIN)
            for n in range(0, IMAGES, PER_STORE):
                eng.dma_start(
                    x1d[:, n * SIDE:(n + PER_STORE) * SIDE, cg * CIN:(cg + 1) * CIN],
                    x[cg * RPAD:cg * RPAD + SIDE, n * SIDE:(n + PER_STORE) * SIDE, :]).then_inc(stored, 16)

        def normalise(vector, n):
            v = pad[:, :, n, HALO:HALO + SIDE]
            return vector.tensor_tensor(v, v, rstd[:, n * SIDE:(n + 1) * SIDE].unsqueeze(1).to_broadcast([P, CIN, SIDE]), ALU.mult)

        @block.sync
        def _(sp):
            for q in range(4):
                sp.dma_start(x[:, q * Q:(q + 1) * Q, :], io["xh"][:, q * Q:(q + 1) * Q, :]).then_inc(x_in[q], 16)
            with sp.Fori(0, CIN // WRING) as it:
                for s in range(WRING):
                    sp.wait_ge(w_free, WRING * it + s + 1)
                    sp.dma_start(wring[:, s, :], io["w0"][bass.ds(WRING * it + s, 1)].rearrange("a p k -> p (a k)")
                                 ).then_inc(w_in[s], 16)
            store(sp, 0)
            store(sp, 1)
            sp.wait_ge(stored, 16 * IMAGES // PER_STORE * CGS)

        @block.gpsimd
        def _(pool):
            nc.gpsimd.memset(pad[:, :, :, 0:HALO], 0.0).then_inc(padded, 1)
            nc.gpsimd.memset(pad[:, :, :, HALO + SIDE:], 0.0).then_inc(padded, 1)
            for q in range(4):
                pool.wait_ge(rstd_ready, q + 1)
                normalise(nc.gpsimd, 4 * q + 3).then_inc(normed, 1)

        @block.scalar
        def _(act):
            act.dma_start(mean_w[:], io["mean_w"]).then_inc(mean_w_in, 16)
            act.wait_ge(x_in[1], 16)
            for dst, name in ((bias[:], "bias0"), (check[:], "check"), (osign[:], "osign")):
                act.dma_start(dst, io[name]).then_inc(consts_in, 16)
            for q in range(4):
                act.wait_ge(centred, q + 1)
                src = pad[:, :, 4 * q:4 * q + 4, HALO:HALO + SIDE].rearrange("p c n w -> p n w c")
                for k in range(4):
                    ins = nc.scalar.activation(sq[:, q * Q + k * SIDE:q * Q + (k + 1) * SIDE, :], src[:, k], ACT.Square)
                ins.then_inc(squared, 1)
            for q in range(4):
                act.wait_ge(var_ready, q + 1)
                cols = slice(q * Q, (q + 1) * Q)
                nc.scalar.activation(rstd[:, cols], rstd[:, cols], ACT.Sqrt).then_inc(std_ready, 1)
            act.wait_ge(normed, 8)
            act.wait_ge(padded, 2)
            with act.Fori(0, CIN // WRING) as it:
                for s in range(WRING):
                    act.wait_ge(w_in[s], 16 * it + 16)
                    act.sem_inc(act_beat, 1)
                    act.wait_ge(acc_ready, WRING * it + s + 1)
                    act.sem_inc(act_beat, 1)
                    nc.scalar.activation(wh[:, s % 2], wring[:, s], ACT.Copy)
                    nc.scalar.activation(ph[:, s % 2], pad[:, bass.ds(WRING * it + s, 1)].rearrange("p a n w -> p (a n) w"), ACT.Copy
                                         ).then_inc(high_ready, 1)
            store(act, 2)
            store(act, 3)

        @block.tensor
        def _(pe):
            pe.wait_ge(mean_w_in, 16)

            def mean(q):
                pe.wait_ge(sums, q + 1)
                nc.tensor.matmul(ps_stat[q][:, 0:Q], mean_w[:], part[:, q * Q:(q + 1) * Q], start=True, stop=True
                                 ).then_inc(mean_ready, 1)

            def variance(q):
                pe.wait_ge(squared, q + 1)
                for c in range(CIN):
                    ins = nc.tensor.matmul(ps_stat[q][:, 0:Q], mean_w[:], sq[:, q * Q:(q + 1) * Q, c], start=c == 0, stop=c == CIN - 1)
                ins.then_inc(var_summed, 1)

            mean(0)
            mean(1)
            for q in range(4):
                if q < 2:
                    mean(q + 2)
                variance(q)
            pe.sem_inc(acc_ready, 2)
            with pe.Fori(0, CIN // WRING) as it:
                for s in range(WRING):
                    pe.wait_ge(split_ready, WRING * it + s + 1)
                    pe.wait_ge(acc_free, WRING * it + s + 1)
                    h = s % 2
                    parts = ((wl, ph), (wh, pl), (wh, ph))
                    for n in range(3 * TAPS):
                        kw, (w, v) = n // 3, parts[n % 3]
                        ins = nc.tensor.matmul(ps[s][:, 0:NW], w[:, h, kw * P:(kw + 1) * P], v[:, h, :, kw:kw + SIDE],
                                               start=n == 0, stop=n == 3 * TAPS - 1)
                    ins.then_inc(acc_ready, 1)

        @block.vector
        def _(dve):
            dve.sem_inc(acc_free, WRING)
            dve.sem_inc(w_free, WRING)
            ch = Chain(dve, chain)

            def add_up(q):
                cols = slice(q * Q, (q + 1) * Q)
                dve.wait_ge(x_in[q], 16)
                nc.vector.tensor_reduce(part[:, cols], x[:, cols, :], AX.X, ALU.add).then_inc(sums, 1)

            def centre(q):
                dve.wait_ge(mean_ready, q + 1)
                for k in range(4):
                    c = slice(q * Q + k * SIDE, q * Q + (k + 1) * SIDE)
                    ins = nc.vector.tensor_tensor(
                        pad[:, :, 4 * q + k, HALO:HALO + SIDE].rearrange("p c w -> p w c"), x[:, c, :],
                        ps_stat[q][:, k * SIDE:(k + 1) * SIDE].unsqueeze(2).to_broadcast([P, SIDE, CIN]), ALU.subtract)
                ins.then_inc(centred, 1)

            add_up(0)
            for q in range(4):
                if q < 3:
                    add_up(q + 1)
                centre(q)
            dve.wait_ge(consts_in, 48)
            for q in range(4):
                cols = slice(q * Q, (q + 1) * Q)
                dve.wait_ge(var_summed, q + 1)
                nc.vector.tensor_scalar(rstd[:, cols], ps_stat[q][:, 0:Q], 1e-6, None, ALU.add).then_inc(var_ready, 1)
                dve.wait_ge(std_ready, q + 1)
                ch.after(nc.vector.reciprocal(rstd[:, cols], rstd[:, cols]))
                ch.after(nc.vector.tensor_tensor(rstd[:, cols], rstd[:, cols], check[:, 0, cols], ALU.mult))
                dve.sem_inc(rstd_ready, 1)
                for k in range(3):
                    ins = normalise(nc.vector, 4 * q + k)
                ins.then_inc(normed, 1)
            dve.wait_ge(normed, 8)

            def split(i, s):
                h = s % 2
                dve.wait_ge(high_ready, i + 1)
                nc.vector.tensor_tensor(wl[:, h], wring[:, s % WRING], wh[:, h].bitcast(F32), ALU.subtract).then_inc(w_free, 1)
                nc.vector.tensor_tensor(pl[:, h], pad[:, bass.ds(i, 1)].rearrange("p a n w -> p (a n) w"), ph[:, h].bitcast(F32),
                                        ALU.subtract).then_inc(split_ready, 1)

            base = ch.n

            def turn(it, last):
                step = Chain(dve, chain, base + 2 * WRING * it)
                for s in range(WRING):
                    i = WRING * it + s
                    if not (last and s == WRING - 1):
                        split(i + 1, s + 1)
                    dve.wait_ge(acc_ready, i + 3)
                    step.after(nc.vector.scalar_tensor_tensor(tmp[:, s % 2, :], ps[s][:, 0:NW], osign[:, s % 2:s % 2 + 1],
                                                              check[:, 1, :], ALU.mult, ALU.mult))
                    dve.sem_inc(acc_free, 1)
                    xr = x[:, :, bass.ds(i, 1)].rearrange("p n a -> p (n a)")
                    step.after(nc.vector.scalar_tensor_tensor(xr, tmp[:, s % 2, :], bias[:, bass.ds(i, 1)], xr, ALU.add, ALU.add))
                    dve.sem_inc(x1_ready, 1)

            split(0, 0)
            with dve.Fori(0, CIN // WRING - 1) as it:
                turn(it, False)
            turn(CIN // WRING - 1, True)


class Routing:

    def __init__(self, nc, ctx):
        sb = lambda n, s, d=F32: ctx.enter_context(nc.sbuf_tensor(n, s, d))
        self.x = sb("x", [P, GROUPS, IG, P])
        self.ident = sb("ident", [P, P])
        self.before = sb("before", [P, P], BF16)
        self.ones = sb("ones", [P, P], BF16)
        self.blank = sb("blank", [P, EXPERTS, PAY])
        self.iota8 = sb("iota8", [P, CHOICES, EXPERTS])
        self.region = sb("region", [P, IG * EXPERTS])
        self.block_no = sb("block_no", [1, TABLE])
        self.dest = sb("dest", [P, GROUPS, CHOICES], I32)
        self.wg = sb("wg", [P, 2, EXPERTS])
        self.table = sb("table", [1, 2, TABLE], I32)
        self.gh = sb("gh", [P, N_UP * PPX], F32R)
        self.gl = sb("gl", [P, N_UP * PPX], F32R)
        self.down = sb("down", [P, N_DOWN * TPX])


class ExpertWeights:

    def __init__(self, nc, ctx, layer):
        sb = lambda n, d=F32: ctx.enter_context(nc.sbuf_tensor(f"{n}_{layer}", [P, EXPERTS * FF], d))
        self.w1h, self.w1l, self.w2 = sb("w1h", F32R), sb("w1l", F32R), sb("w2")
        self.w1f = self.w1l[:].bitcast(F32)


def weights_load(wt, eng, io, layer, w_in):
    k2 = FF // P if layer == 0 else FF // P // 2
    eng.dma_start(wt.w1f, io[f"w1_{layer}"].rearrange("p e f -> p (e f)")).then_inc(w_in, 16)
    eng.dma_start(wt.w2[:].rearrange("p (e k) -> p e k", e=EXPERTS)[:, :, 0:k2 * P],
                  io[f"w2_{layer}"].rearrange("p e c d -> p e (c d)")).then_inc(w_in, 16)


class Norm:

    def __init__(self, nc, ctx, sem, name, eps):
        sb = lambda n, s: ctx.enter_context(nc.sbuf_tensor(f"{name}_{n}", s, F32))
        self.nc, self.eps = nc, eps
        self.stats, self.mv = sb("stats", [P, IG, 6]), sb("mv", [P, IG, 2])
        self.rstd = sb("rstd", [P, IG])
        self.chain, self.beat = sem(f"{name}_chain"), sem(f"{name}_beat")
        self.var_ready, self.std_ready, self.applied = (sem(f"{name}_{n}") for n in ("var", "std", "applied"))


def norm_measure(m, dve, ig, q, x):
    nc, px, g = m.nc, pixels(q), QT * ig + q
    ch = Chain(dve, m.chain, NORM_STEPS * g)
    for t in range(IG):
        ins = nc.vector.bn_stats(m.stats[0:px, t, :], x[:, t, :])
    ch.after(ins, m.beat)
    for t in range(IG):
        ins = nc.vector.bn_aggr(m.mv[0:px, t, :], m.stats[0:px, t, :])
    ch.after(ins)
    nc.vector.tensor_scalar(m.rstd[0:px], m.mv[0:px, :, 1], m.eps, None, ALU.add).then_inc(m.var_ready, 1)


def norm_root(m, act, ig, q):
    px = pixels(q)
    need(act, m.var_ready, QT * ig + q + 1)
    m.nc.scalar.activation(m.rstd[0:px], m.rstd[0:px], ACT.Sqrt).then_inc(m.std_ready, 1)


def norm_scale(m, dve, ig, q):
    nc, px, g = m.nc, pixels(q), QT * ig + q
    ch = Chain(dve, m.chain, NORM_STEPS * g + 2)
    need(dve, m.std_ready, g + 1)
    ch.after(nc.vector.reciprocal(m.rstd[0:px], m.rstd[0:px]))


def norm_apply(m, dve, ig, q, out, x):
    px = pixels(q)
    for t in range(IG):
        ins = m.nc.vector.tensor_scalar(out[:, t, :], x[:, t, :], m.mv[0:px, t, 0:1], m.rstd[0:px, t:t + 1],
                                           ALU.subtract, ALU.mult)
    ins.then_inc(m.applied, 1)


class Router:

    def __init__(self, nc, ctx, sem, r, layer, xs):
        sb = lambda n, s, d=F32: ctx.enter_context(nc.sbuf_tensor(f"r{layer}_{n}", s, d))
        ps = lambda n: ctx.enter_context(nc.psum_tensor(f"r{layer}_ps_{n}", [P, 512], F32))
        self.nc, self.r, self.layer, self.xs = nc, r, layer, xs
        self.norm = Norm(nc, ctx, sem, f"ln{layer}", 1e-5)
        self.xn = sb("xn", [P, QT, 2, IG, PAY])
        self.xnt = sb("xnt", [P, IG, P])
        self.top, self.top_at = sb("top", [P, IG, 8]), sb("top_at", [P, IG, 8], U32)
        self.at, self.gap, self.ex, self.den = sb("at", [P, CHOICES]), sb("gap", [P, IG]), sb("ex", [P, IG]), sb("den", [P, IG])
        self.onehot, self.picked = sb("onehot", [P, IG, 2, EXPERTS]), sb("picked", [P, IG, EXPERTS], BF16)
        self.earlier = sb("earlier", [P, EXPERTS], BF16)
        self.group_sum = sb("group_sum", [P, EXPERTS])
        self.rank, self.prod = sb("rank", [P, IG * EXPERTS]), sb("prod", [P, IG, 2, EXPERTS])
        self.slot_f, self.slot = sb("slot_f", [P, CHOICES]), sb("slot", [P, QT, CHOICES], I32)
        self.count, self.tail_i = sb("count", [P, EXPERTS]), sb("tail_i", [1, EXPERTS], I32)
        self.nblk_i, self.nblk, self.upto = sb("nblk_i", [P, EXPERTS], I32), sb("nblk", [P, EXPERTS]), sb("upto", [P, EXPERTS])
        self.passed = sb("passed", [1, TABLE, EXPERTS])
        self.t_e, self.t_prev, self.t_j, self.t_f = (sb(f"tab{i}", [1, TABLE]) for i in range(4))
        self.ps_t, self.ps_l, self.ps_rank = ps("t"), ps("l"), ps("rank")
        self.scattered = [sem(f"scattered{q}") for q in range(QT)]
        (self.chain, self.pool_beat, self.xn_ready, self.turned, self.xnt_ready, self.logits_ready,
         self.picked_ready, self.gap_ready, self.exp_ready, self.rank_ready, self.slot_ready, self.counted,
         self.tail_ready, self.tails, self.cleared, self.dve_beat) = (
            sem(f"route_{n}") for n in ("chain", "pool_beat", "xn", "turned", "xnt", "logits", "picked", "gap", "exp",
                             "rank", "slot", "counted", "tail", "tails", "cleared", "dve_beat"))


def route_clear(ro, pool):
    ro.nc.gpsimd.memset(ro.xn[:], 0.0).then_inc(ro.cleared, 1)
    ro.nc.gpsimd.memset(ro.earlier[:], 0.0).then_inc(ro.cleared, 1)


def route_normalise(ro, dve, ig, q):
    px = pixels(q)
    if isinstance(ig, int) and ig == 0 and q == 0:
        dve.wait_ge(ro.cleared, 2)
    need(dve, ro.scattered[q], 16 * CHOICES * ig)
    ro.nc.vector.tensor_copy(
        ro.xn[0:px, q, :, :, DEST].bitcast(I32),
        ro.r.dest[0:px, bass.ds(QT * ig + q, 1), :].rearrange("p a (t k) -> p k (a t)", k=2))
    norm_apply(ro.norm, dve, ig, q, ro.xn[0:px, q, 0, :, 0:P],
                    ro.r.x[0:px, bass.ds(QT * ig + q, 1)].rearrange("p a t c -> p (a t) c"))


def route_copy_rows(ro, act, ig, q):
    px = pixels(q)
    need(act, ro.norm.applied, QT * ig + q + 1)
    ro.nc.scalar.activation(ro.xn[0:px, q, 1, :, 0:P], ro.xn[0:px, q, 0, :, 0:P], ACT.Copy).then_inc(ro.xn_ready, 1)


def route_turn(ro, pe, ig, q):
    px, g = pixels(q), QT * ig + q
    need(pe, ro.norm.applied, g + 1)
    need(pe, ro.xnt_ready, g)
    for t in range(IG):
        ins = ro.nc.tensor.transpose(ro.ps_t[:, t * P:t * P + px], ro.xn[0:px, q, 0, t, 0:P], ro.r.ident[0:px, 0:px])
    ins.then_inc(ro.turned, 1)


def route_copy_turned(ro, act, ig, q):
    px, g = pixels(q), QT * ig + q
    need(act, ro.turned, g + 1)
    need(act, ro.logits_ready, g)
    ro.nc.scalar.activation(ro.xnt[:, :, 0:px], ro.ps_t[:].rearrange("p (t x) -> p t x", x=P)[:, :, 0:px], ACT.Copy
                              ).then_inc(ro.xnt_ready, 1)


def route_logits(ro, pe, ig, q):
    px, g = pixels(q), QT * ig + q
    need(pe, ro.xnt_ready, g + 1)
    need(pe, ro.picked_ready, g)
    for t in range(IG):
        ins = ro.nc.tensor.matmul(ro.ps_l[0:px, t * EXPERTS:(t + 1) * EXPERTS], ro.xnt[:, t, 0:px],
                                    ro.r.wg[:, ro.layer, :], start=True, stop=True)
    ins.then_inc(ro.logits_ready, 1)


def route_pick(ro, dve, ig, q):
    nc, px, g = ro.nc, pixels(q), QT * ig + q
    ch = Chain(dve, ro.chain, (PICK_STEPS + PLACE_STEPS) * g)
    need(dve, ro.logits_ready, g + 1, ro.dve_beat)
    cols = lambda t: ro.ps_l[0:px, t * EXPERTS:(t + 1) * EXPERTS]
    for t in range(IG):
        ins = nc.vector.max(ro.top[0:px, t, :], cols(t))
    ch.after(ins, ro.dve_beat)
    for t in range(IG):
        ins = nc.vector.max_index(ro.top_at[0:px, t, :], ro.top[0:px, t, :], cols(t))
    nc.vector.tensor_tensor(ro.gap[0:px], ro.top[0:px, :, 1], ro.top[0:px, :, 0], ALU.subtract).then_inc(ro.gap_ready, 1)
    ch.after(ins)
    ch.after(nc.vector.tensor_copy(ro.at[0:px].rearrange("p (t k) -> p t k", k=2), ro.top_at[0:px, :, 0:2]))
    ch.after(nc.vector.tensor_tensor(ro.onehot[0:px].rearrange("p t k e -> p (t k) e"), ro.r.iota8[0:px],
                                     ro.at[0:px].unsqueeze(2).to_broadcast([px, CHOICES, EXPERTS]), ALU.is_equal))
    ch.after(nc.vector.tensor_tensor(ro.picked[0:px], ro.onehot[0:px, :, 0, :], ro.onehot[0:px, :, 1, :], ALU.add))
    dve.sem_inc(ro.picked_ready, 1)
    nc.vector.tensor_reduce(ro.group_sum[0:px], ro.picked[0:px].rearrange("p t e -> p e t"), AX.X, ALU.add
                            ).then_inc(ro.chain, 1)


def route_exponent(ro, act, ig, q):
    px, g = pixels(q), QT * ig + q
    need(act, ro.gap_ready, g + 1)
    ro.nc.scalar.activation(ro.ex[0:px], ro.gap[0:px], ACT.Exp).then_inc(ro.exp_ready, 1)


def route_ranks(ro, pe, ig, q):
    nc, px, g = ro.nc, pixels(q), QT * ig + q
    need(pe, ro.picked_ready, g + 1)
    out = lambda t: ro.ps_rank[0:px, t * EXPERTS:IG * EXPERTS]
    nc.tensor.matmul(out(0), ro.r.before[0:px, 0:px], ro.picked[0:px].rearrange("p t e -> p (t e)"), start=True, stop=False)
    for t in range(IG - 1):
        nc.tensor.matmul(out(t + 1), ro.r.ones[0:px, 0:px],
                         ro.picked[0:px, t, :].unsqueeze(1).to_broadcast([px, IG - 1 - t, EXPERTS]), start=False, stop=False)
    nc.tensor.matmul(out(0), ro.r.ones[:, 0:px], ro.earlier[:].unsqueeze(1).to_broadcast([P, IG, EXPERTS]),
                     start=False, stop=True).then_inc(ro.rank_ready, 1)


def route_place(ro, dve, ig, q):
    nc, px, g = ro.nc, pixels(q), QT * ig + q
    ch = Chain(dve, ro.chain, (PICK_STEPS + PLACE_STEPS) * g + PICK_STEPS)
    need(dve, ro.exp_ready, g + 1)
    nc.vector.tensor_scalar(ro.den[0:px], ro.ex[0:px], 1.0, None, ALU.add)
    need(dve, ro.rank_ready, g + 1)
    need(dve, ro.chain, ch.base)
    nc.vector.tensor_tensor(ro.earlier[0:px], ro.earlier[0:px], ro.group_sum[0:px], ALU.add)
    ch.after(nc.vector.tensor_tensor(ro.rank[0:px], ro.ps_rank[0:px, 0:IG * EXPERTS], ro.r.region[0:px], ALU.add))
    nc.vector.reciprocal(ro.xn[0:px, q, 0, :, WEIGHT], ro.den[0:px])
    rank = ro.rank[0:px].rearrange("p (t e) -> p t e", e=EXPERTS).unsqueeze(2).to_broadcast([px, IG, 2, EXPERTS])
    ch.after(nc.vector.tensor_tensor(ro.prod[0:px], ro.onehot[0:px], rank, ALU.mult))
    nc.vector.tensor_tensor(ro.xn[0:px, q, 1, :, WEIGHT], ro.ex[0:px], ro.xn[0:px, q, 0, :, WEIGHT], ALU.mult)
    ch.after(nc.vector.tensor_reduce(ro.slot_f[0:px], ro.prod[0:px].rearrange("p t k e -> p (t k) e"), AX.X, ALU.add))
    need(dve, ro.scattered[q], 16 * CHOICES * ig)
    ch.after(nc.vector.tensor_copy(ro.slot[0:px, q], ro.slot_f[0:px]))
    dve.sem_inc(ro.slot_ready, 1)


def route_scatter(ro, pool, ig, q):
    px, g = pixels(q), QT * ig + q
    need(pool, ro.xn_ready, g + 1, ro.pool_beat)
    need(pool, ro.slot_ready, g + 1, ro.pool_beat)
    for t in range(IG):
        for k in range(2):
            c = 2 * t + k
            ro.nc.gpsimd.indirect_dma_start(ro.xs, bass.IndirectOffsetOnAxis(ap=ro.slot[0:px, q, c:c + 1], axis=0),
                                              ro.xn[0:px, q, k, t, :], None).then_inc(ro.scattered[q], 16)


def route_count_all(ro, pe):
    pe.wait_ge(ro.chain, (PICK_STEPS + PLACE_STEPS) * GROUPS)
    ro.nc.tensor.matmul(ro.ps_rank[:, 0:EXPERTS], ro.r.ones[:], ro.earlier[:], start=True, stop=True
                          ).then_inc(ro.counted, 1)


def route_make_table(ro, dve):
    nc, r = ro.nc, ro.r
    ch = Chain(dve, ro.chain, (PICK_STEPS + PLACE_STEPS) * GROUPS)
    dve.wait_ge(ro.counted, 1)
    ch.after(nc.vector.tensor_copy(ro.count[:], ro.ps_rank[:, 0:EXPERTS]))
    nc.vector.tensor_tensor(ro.tail_i[:], ro.count[0:1], r.region[0:1, 0:EXPERTS], ALU.add).then_inc(ro.tail_ready, 1)
    ch.after(nc.vector.tensor_scalar(ro.nblk_i[:], ro.count[:], float(P - 1), None, ALU.add))
    ch.after(nc.vector.tensor_scalar(ro.nblk_i[:], ro.nblk_i[:], 7, None, ALU.arith_shift_right))
    ch.after(nc.vector.tensor_copy(ro.nblk[:], ro.nblk_i[:]))
    ch.after(nc.vector.tensor_copy(ro.upto[:, 0:1], ro.nblk[:, 0:1]))
    for e in range(1, EXPERTS):
        ch.after(nc.vector.tensor_tensor(ro.upto[:, e:e + 1], ro.upto[:, e - 1:e], ro.nblk[:, e:e + 1], ALU.add))
    wide = lambda v: v[0:1, :].unsqueeze(1).to_broadcast([1, TABLE, EXPERTS])
    block_no = r.block_no[:].unsqueeze(2).to_broadcast([1, TABLE, EXPERTS])
    ch.after(nc.vector.tensor_tensor(ro.passed[:], block_no, wide(ro.upto), ALU.is_ge))
    t_e, t_prev, t_j, t_f = ro.t_e, ro.t_prev, ro.t_j, ro.t_f
    ch.after(nc.vector.tensor_reduce(t_e[:], ro.passed[:], AX.X, ALU.add))
    ch.after(nc.vector.tensor_tensor(ro.passed[:], ro.passed[:], wide(ro.nblk), ALU.mult))
    ch.after(nc.vector.tensor_reduce(t_prev[:], ro.passed[:], AX.X, ALU.add))
    ch.after(nc.vector.tensor_tensor(t_j[:], r.block_no[:], t_prev[:], ALU.subtract))
    ch.after(nc.vector.tensor_scalar(t_j[:], t_j[:], float(P), None, ALU.mult))
    ch.after(nc.vector.scalar_tensor_tensor(t_f[:], t_e[:], float(REGION), t_j[:], ALU.mult, ALU.add))
    nc.vector.tensor_copy(r.table[:, 0, :], t_f[:])
    ch.after(nc.vector.tensor_scalar(t_e[:], t_e[:], float(EXPERTS - 1), None, ALU.min))
    n, shift = TABLE, 1
    while shift < 8:
        n -= shift
        ch.after(nc.vector.scalar_tensor_tensor(t_e[:, 0:n], t_e[:, shift:shift + n], float(EXPERTS ** shift), t_e[:, 0:n],
                                                ALU.mult, ALU.add))
        shift *= 2
    nc.vector.tensor_copy(r.table[:, 1, 0:n], t_e[:, 0:n])


def route_store_tails(ro, sp):
    sp.wait_ge(ro.tail_ready, 1)
    for e in range(EXPERTS):
        end = sp.value_load(ro.tail_i[0:1, e:e + 1], min_val=0, max_val=EXPERTS * REGION - P)
        sp.dma_start(ro.xs[bass.ds(end, P), :], ro.r.blank[:, e, :]).then_inc(ro.tails, 16)
    sp.wait_ge(ro.tails, 16 * EXPERTS)


def route_finish(ro, pool):
    for q in range(QT):
        pool.wait_ge(ro.scattered[q], 16 * CHOICES * IMAGE_GROUPS)


def route0_phase(nc, io, r, wt, xs, src):
    with ExitStack() as ctx:
        sem = ctx.enter_context(stage_semaphores(nc, "r0_"))
        ro = Router(nc, ctx, sem, r, 0, xs)
        fa, fb = (ctx.enter_context(nc.sbuf_tensor(n, [P, N_UP * PPX], F32)) for n in ("factor_a", "factor_b"))
        before_f = ctx.enter_context(nc.sbuf_tensor("before_f", [P, P], F32))
        down_b = ctx.enter_context(nc.sbuf_tensor("down_b", [P, N_DOWN * TPX], F32))
        x_in = [sem(f"x_in{q}") for q in range(QT)]
        consts_in, blank_in, init, w_in, w_split, factors_in, g_ready, gh_ready, blank_out = (
            sem(n) for n in ("consts_in", "blank_in", "init", "w_in", "w_split", "factors_in", "g", "gh", "blank_out"))
        block = ctx.enter_context(nc.Block())
        LAST = (IMAGE_GROUPS - 1, QT - 1)

        @block.sync
        def _(sp):
            def load(ig, q):
                px = pixels(q)
                need(sp, ro.norm.applied, QT * (ig - 1) + q + 1)
                for row in range(px // SIDE):
                    sp.dma_start(r.x[row * SIDE:(row + 1) * SIDE, bass.ds(QT * ig + q, 1)].rearrange("p a t c -> p (a t) c"),
                                 src[ROWS * q + row].rearrange("(n w) c -> w n c", w=SIDE)[:, bass.ds(IG * ig, IG), :]
                                 ).then_inc(x_in[q], 16)
            def load_weights():
                for dst, name in ((fa, "up_a"), (fb, "up_b"), (r.down, "down_a"), (down_b, "down_b")):
                    sp.dma_start(dst[:], io[name].rearrange("p m k -> p (m k)")).then_inc(factors_in, 16)
                weights_load(wt, sp, io, 0, w_in)
            groups(sp, load, load_weights)
            sp.wait_ge(blank_in, 16)
            route_store_tails(ro, sp)

        @block.scalar
        def _(act):
            for dst, name in ((r.ident[:], "ident"), (before_f[:], "before"), (r.region[:], "region"),
                              (r.wg[:, 0, :], "wg0"), (r.wg[:, 1, :], "wg1")):
                act.dma_start(dst, io[name]).then_inc(consts_in, 16)
            act.dma_start(r.iota8[:].rearrange("p a e -> p (a e)"), io["iota8"]).then_inc(consts_in, 16)
            act.dma_start(r.block_no[:], io["block_no"]).then_inc(consts_in, 16)
            act.dma_start(r.dest[:], io["dest"]).then_inc(consts_in, 16)
            act.dma_start(r.blank[:].rearrange("p e c -> p (e c)"), io["blank"]).then_inc(blank_in, 16)
            act.dma_start(xs[EXPERTS * REGION:, :], io["blank_rows"]).then_inc(blank_out, 16)

            def step(ig, q):
                last = before(ig, q)
                norm_root(ro.norm, act, ig, q)
                if last:
                    route_exponent(ro, act, *last)
                route_copy_rows(ro, act, ig, q)
                route_copy_turned(ro, act, ig, q)
            groups(act, step)
            route_exponent(ro, act, *LAST)
            act.wait_ge(w_in, 32)
            nc.scalar.activation(wt.w1h[:], wt.w1f, ACT.Copy).then_inc(w_split, 1)
            act.wait_ge(g_ready, 1)
            nc.scalar.activation(r.gh[:], fa[:], ACT.Copy).then_inc(gh_ready, 1)
            act.wait_ge(blank_out, 16)

        @block.gpsimd
        def _(pool):
            nc.gpsimd.memset(r.ones[:], 1.0).then_inc(init, 1)
            route_clear(ro, pool)
            groups(pool, lambda ig, q: route_scatter(ro, pool, ig, q))
            route_finish(ro, pool)

        @block.tensor
        def _(pe):
            pe.wait_ge(consts_in, 16 * 8)
            pe.wait_ge(init, 2)

            def step(ig, q):
                last = before(ig, q)
                if last:
                    route_ranks(ro, pe, *last)
                route_turn(ro, pe, ig, q)
                route_logits(ro, pe, ig, q)
            groups(pe, step)
            route_ranks(ro, pe, *LAST)
            route_count_all(ro, pe)

        @block.vector
        def _(dve):
            dve.wait_ge(consts_in, 16 * 8)
            nc.vector.tensor_copy(r.before[:], before_f[:]).then_inc(init, 1)

            def step(ig, q):
                last = before(ig, q)
                need(dve, x_in[q], 16 * (pixels(q) // SIDE) * (ig + 1), ro.norm.beat)
                norm_measure(ro.norm, dve, ig, q, r.x[0:pixels(q), bass.ds(QT * ig + q, 1)].rearrange("p a t c -> p (a t) c"))
                if last:
                    route_pick(ro, dve, *last)
                norm_scale(ro.norm, dve, ig, q)
                route_normalise(ro, dve, ig, q)
                if last:
                    route_place(ro, dve, *last)
            groups(dve, step)
            route_pick(ro, dve, *LAST)
            dve.wait_ge(factors_in, 64)
            nc.vector.scalar_tensor_tensor(fa[:], fa[:], 4.0, fb[:], ALU.mult, ALU.mult).then_inc(g_ready, 1)
            route_place(ro, dve, *LAST)
            route_make_table(ro, dve)
            nc.vector.tensor_tensor(r.down[:], r.down[:], down_b[:], ALU.mult)
            dve.wait_ge(gh_ready, 1)
            nc.vector.tensor_tensor(r.gl[:], fa[:], r.gh[:].bitcast(F32), ALU.subtract)
            dve.wait_ge(w_split, 1)
            nc.vector.tensor_tensor(wt.w1l[:], wt.w1f, wt.w1h[:].bitcast(F32), ALU.subtract)


def expert_phase(nc, r, wt, layer, xs, ys):
    chunks = FF // P if layer == 0 else FF // P // 2
    HID = chunks * P
    with ExitStack() as ctx:
        sb = lambda n, s, d=F32: ctx.enter_context(nc.sbuf_tensor(f"e{layer}_{n}", s, d))
        sem = ctx.enter_context(stage_semaphores(nc, f"e{layer}_"))
        ps = lambda n: [ctx.enter_context(nc.psum_tensor(f"e{layer}_ps_{n}{i}", [P, 512], F32)) for i in range(2)]
        U, AHEAD = 8, 7
        xg = sb("xg", [P, U, PAY])
        dest, weight = sb("dest", [P, U], I32), sb("weight", [P, U])
        xh, xl = sb("xh", [P, 2, P], F32R), sb("xl", [P, 2, P], F32R)
        gate = sb("gate", [P, 2, FF // 2]) if layer else None
        h, ht, y = sb("h", [P, 2, HID]), sb("ht", [P, 2, HID]), sb("y", [P, U, P])
        ps_x, ps_h, ps_ht, ps_y = ps("x"), ps("h"), ps("ht"), ps("y")
        x_in = [sem(f"x_in{s}") for s in range(U)]
        stored = [sem(f"stored{s}") for s in range(U)]
        x_turned, x_split, h_ready, gated, hid_ready, h_turned, ht_ready, y_done, y_ready, hi_done, pool_beat = (
            sem(n) for n in ("x_turned", "x_split", "h_ready", "gated", "hid_ready", "h_turned", "ht_ready", "y_done",
                             "y_ready", "hi_done", "pool_beat"))
        block = ctx.enter_context(nc.Block())
        STEPS = BLOCKS // U

        def steps(eng, step):
            for s in range(U):
                step(0, s, True)
            with eng.Fori(1, STEPS) as it:
                for s in range(U):
                    step(it, s, False)

        @block.sync
        def _(sp):
            row = lambda b: sp.value_load(r.table[0:1, 0, bass.ds(b, 1)], min_val=0, max_val=EXPERTS * REGION + (SPARE - 1) * P)

            def load(b, slot, again):
                start = row(b)
                if again:
                    sp.wait_ge(x_split, b - U + 1)
                sp.dma_start(xg[:, slot, :], xs[bass.ds(start, P), :]).then_inc(x_in[slot], 16)

            for s in range(AHEAD):
                load(s, s, False)

            def step(it, s, first):
                b = U * it + s
                load(b + AHEAD, (s + AHEAD) % U, not first or s + AHEAD >= U)
            steps(sp, step)
            for s in range(U):
                sp.wait_ge(x_in[s], 16 * (STEPS + (1 if s < AHEAD else 0)))

        @block.gpsimd
        def _(pool):
            def step(it, s, first):
                pool.wait_ge(y_ready, U * it + s + 1)
                pool.sem_inc(pool_beat, 1)
                nc.gpsimd.indirect_dma_start(ys, bass.IndirectOffsetOnAxis(ap=dest[:, s:s + 1], axis=0),
                                             y[:, s, :], None).then_inc(stored[s], 16)
            steps(pool, step)
            for s in range(U):
                pool.wait_ge(stored[s], 16 * STEPS)

        @block.tensor
        def _(pe):
            def experts_from(b):
                return pe.value_load(r.table[0:1, 1, bass.ds(b, 1)], min_val=0, max_val=EXPERTS ** 8 - 1)

            def weights_of(experts, n):
                return ((experts >> (3 * n)) & (EXPERTS - 1)) * FF

            def turn_x(b, s, turn_no, early):
                pe.wait_ge(x_in[s % U], 16 * (turn_no + 1))
                if not early:
                    pe.wait_ge(x_split, b - 1)
                nc.tensor.transpose(ps_x[s % 2][:, 0:P], xg[:, s % U, 0:P], r.ident[:]).then_inc(x_turned, 1)

            def first_product(b, s, w, early):
                pe.wait_ge(x_split, b + 1)
                if not early:
                    pe.wait_ge(hid_ready, b - 1)
                i = s % 2
                nc.tensor.matmul(ps_h[i][:], xl[:, i, :], wt.w1h[:, bass.ds(w, FF)], start=True, stop=False)
                nc.tensor.matmul(ps_h[i][:], xh[:, i, :], wt.w1l[:, bass.ds(w, FF)], start=False, stop=False)
                nc.tensor.matmul(ps_h[i][:], xh[:, i, :], wt.w1h[:, bass.ds(w, FF)], start=False, stop=True
                                 ).then_inc(h_ready, 1)

            def turn_h(b, s, early):
                pe.wait_ge(hid_ready, b + 1)
                if not early:
                    pe.wait_ge(ht_ready, b - 1)
                for c in range(chunks):
                    ins = nc.tensor.transpose(ps_ht[s % 2][:, c * P:(c + 1) * P], h[:, s % 2, c * P:(c + 1) * P], r.ident[:])
                ins.then_inc(h_turned, 1)

            def second_product(b, s, w, early):
                pe.wait_ge(ht_ready, b + 1)
                if not early:
                    pe.wait_ge(y_ready, b - 1)
                for c in range(chunks):
                    ins = nc.tensor.matmul(ps_y[s % 2][:, 0:P], ht[:, s % 2, c * P:(c + 1) * P],
                                           wt.w2[:, bass.ds(w + c * P, P)], start=c == 0, stop=c == chunks - 1)
                ins.then_inc(y_done, 1)

            w = {}
            experts = experts_from(0)
            for s in range(2):
                w[s + 1] = weights_of(experts, s)
            for s in range(2):
                turn_x(s, s, 0, True)
            for s in range(2):
                first_product(s, s, w[s + 1], True)
            turn_x(2, 2, 0, False)

            def step(it, s, first):
                b = U * it + s
                turn_h(b, s, first and s < 2)
                turn_x(b + 3, s + 3, it + (1 if s + 3 >= U else 0), False)
                if s == 0:
                    begin = 1 if first else 0
                    experts = experts_from(0 if first else b - 1)
                    for n in range(8):
                        w[begin + n] = weights_of(experts, n)
                if not (first and s == 0):
                    second_product(b - 1, s - 1, w[s], first and s < 3)
                first_product(b + 2, s + 2, w[s + 3], False)
                if s == 3:
                    begin = 9 if first else 8
                    experts = experts_from(8 if first else b + 4)
                    for n in range(begin, U + 3):
                        w[n] = weights_of(experts, n - begin)
            steps(pe, step)
            second_product(BLOCKS - 1, U - 1, w[U], False)

        @block.scalar
        def _(act):
            def activate(b, s, early):
                act.wait_ge(h_ready, b + 1)
                i = s % 2
                if layer:
                    if not early:
                        act.wait_ge(hid_ready, b - 1)
                    nc.scalar.activation(gate[:, i, :], ps_h[i][:, 0:HID], ACT.Silu).then_inc(gated, 1)
                else:
                    if not early:
                        act.wait_ge(h_turned, b - 1)
                    nc.scalar.activation(h[:, i, :], ps_h[i][:], ACT.Silu).then_inc(hid_ready, 1)

            def answer(b, s):
                act.wait_ge(y_done, b + 1)
                nc.scalar.activation(y[:, s % U, :], ps_y[s % 2][:, 0:P], ACT.Copy,
                                     scale=weight[:, s % U:s % U + 1]).then_inc(y_ready, 1)

            activate(0, 0, True)
            activate(1, 1, True)

            def step(it, s, first):
                b = U * it + s
                if not (first and s == 0):
                    answer(b - 1, s - 1)
                activate(b + 2, s + 2, False)
            steps(act, step)
            answer(BLOCKS - 1, U - 1)

        @block.vector
        def _(dve):
            def split(b, s, turn_no, early):
                dve.wait_ge(x_turned, b + 1)
                if not early:
                    dve.wait_ge(h_ready, b - 1)
                i, slot = s % 2, s % U
                if not isinstance(turn_no, int) or turn_no:
                    dve.wait_ge(stored[slot], 16 * turn_no)
                nc.vector.tensor_copy(dest[:, slot:slot + 1], xg[:, slot, DEST:DEST + 1].bitcast(I32))
                nc.vector.tensor_copy(weight[:, slot:slot + 1], xg[:, slot, WEIGHT:WEIGHT + 1])
                nc.vector.tensor_copy(xh[:, i, :], ps_x[i][:, 0:P]).then_inc(hi_done, 1)
                dve.wait_ge(hi_done, b + 1)
                nc.vector.tensor_tensor(xl[:, i, :], ps_x[i][:, 0:P], xh[:, i, :].bitcast(F32), ALU.subtract
                                        ).then_inc(x_split, 1)

            def gate_product(b, s, early):
                dve.wait_ge(gated, b + 1)
                if not early:
                    dve.wait_ge(h_turned, b - 1)
                i = s % 2
                nc.vector.tensor_tensor(h[:, i, :], gate[:, i, :], ps_h[i][:, HID:2 * HID], ALU.mult
                                        ).then_inc(hid_ready, 1)

            split(0, 0, 0, True)
            split(1, 1, 0, True)
            split(2, 2, 0, False)
            if layer:
                gate_product(0, 0, True)

            def step(it, s, first):
                b = U * it + s
                dve.wait_ge(h_turned, b + 1)
                if not (first and s < 2):
                    dve.wait_ge(y_done, b - 1)
                nc.vector.tensor_copy(ht[:, s % 2, :], ps_ht[s % 2][:, 0:HID]).then_inc(ht_ready, 1)
                if layer:
                    gate_product(b + 1, s + 1, first and s == 0)
                split(b + 3, s + 3, it + (s + 3) // U, False)
            steps(dve, step)
            if layer:
                gate_product(BLOCKS + 1, U + 1, False)


class Answers:

    def __init__(self, nc, ctx, sem, r, ys, ring):
        self.nc, self.r, self.ring = nc, r, ring
        self.places = ys[0:ANSWERS].rearrange("(g p n) c -> p g (n c)", p=TPX, n=CHOICES)
        self.y = ctx.enter_context(nc.sbuf_tensor(f"answers_{ring}", [P, ring, IG, 2, P], F32))
        self.y_in = [sem(f"y_in{i}") for i in range(ring)]
        self.half, self.added, self.beat = sem("half"), sem("added"), sem("add_beat")


def answers_load(an, sp, ig, q):
    px, s = pixels(q), q % an.ring
    need(sp, an.added, QT * ig + last_user(q, an.ring, QT) + 1)
    sp.dma_start(an.y[0:px, s].rearrange("p t k c -> p (t k c)"),
                 an.places[0:px, bass.ds(QT * ig + q, 1), :].rearrange("p a n -> p (a n)")).then_inc(an.y_in[s], 16)


def answers_add(an, eng, vector, ig, q):
    px, s, g = pixels(q), q % an.ring, QT * ig + q
    per_turn = len(range(s, QT, an.ring))
    x = an.r.x[0:px, bass.ds(g, 1)].rearrange("p a t c -> p (a t) c")
    need(eng, an.y_in[s], 16 * (per_turn * ig + q // an.ring + 1), an.beat)
    vector.tensor_tensor(x, x, an.y[0:px, s, :, 0, :], ALU.add).then_inc(an.half, 1)
    need(eng, an.half, g + 1, an.beat)
    vector.tensor_tensor(x, x, an.y[0:px, s, :, 1, :], ALU.add).then_inc(an.added, 1)


def conv1_phase(nc, io, r, wt, xs, ys):
    with ExitStack() as ctx:
        sb = lambda n, s, d=F32: ctx.enter_context(nc.sbuf_tensor(f"c1_{n}", s, d))
        sem = ctx.enter_context(stage_semaphores(nc, "c1_"))
        ro = Router(nc, ctx, sem, r, 1, xs)
        an = Answers(nc, ctx, sem, r, ys, 2)
        lnc = Norm(nc, ctx, sem, "lnc", 1e-6)
        R = 10
        xf = sb("xf", [P, 2, NC])
        xh, xl = sb("xh", [P, QT, NC], F32R), sb("xl", [P, QT, NC], F32R)
        a, c = sb("a", [P, 2, NC]), sb("c", [P, R, NC])
        ps_y = [ctx.enter_context(nc.psum_tensor(f"c1_py{i}", [P, 512], F32)) for i in range(2)]
        ps_z = [ctx.enter_context(nc.psum_tensor(f"c1_pz{i}", [P, 512], F32)) for i in range(3)]
        (xf_clear, bias_in, bias_high, bias_split, xh_ready, xl_ready, y_raw, y_copied, y_leaky, y_clip, down_done,
         z_added, w_in, w_split) = (
            sem(n) for n in ("xf_clear", "bias_in", "bias_high", "bias_split", "xh", "xl", "y_raw", "y_copied", "y_leaky", "y_clip",
                             "down_done", "z_added", "w_in", "w_split"))
        AHEAD = 7
        LAG = 8
        up_w = lambda m: slice(m * PPX, (m + 1) * PPX)
        last_pair = lambda q: min(ROWS * q + 2 * ROWS - 1, PAIRS - 1)
        MEASURE, ROOT, SCALE, HIGH, SPLIT = ([ROWS * q - n for q in range(QT)] for n in (8, 6, 5, 4, 3))
        DOWN = [last_pair(q) + LAG for q in range(QT)]
        after = lambda n: [s + n for s in DOWN]
        block = ctx.enter_context(nc.Block())

        def due(it, n, steps):
            found = [(it - s // PAIRS, q) for q, s in enumerate(steps) if s % PAIRS == n]
            return [(ig, q) for ig, q in found if not isinstance(ig, int) or 0 <= ig < IMAGE_GROUPS]

        def pair(it, n):
            ig, p = it + n // PAIRS, n % PAIRS
            return [(ig, p)] if not isinstance(ig, int) or 0 <= ig < IMAGE_GROUPS else []

        def turns(eng, step):
            def turn(it):
                for n in range(PAIRS):
                    step(it, n)
            turn(-1)
            turn(0)
            with eng.Fori(1, IMAGE_GROUPS - 1) as it:
                turn(it)
            turn(IMAGE_GROUPS - 1)
            turn(IMAGE_GROUPS)

        @block.sync
        def _(sp):
            sp.wait_ge(xf_clear, 1)
            for i in range(2):
                sp.dma_start(xf[TPX:TPX + 1, i], io["bias1"]).then_inc(bias_in, 16)
            for q in range(2):
                answers_load(an, sp, 0, q)
            weights_load(wt, sp, io, 1, w_in)
            for q in range(2, QT):
                answers_load(an, sp, 0, q)
            with sp.Fori(1, IMAGE_GROUPS) as ig:
                for q in range(QT):
                    answers_load(an, sp, ig, q)
            route_store_tails(ro, sp)

        @block.gpsimd
        def _(pool):
            nc.gpsimd.memset(xf[:], 0.0).then_inc(xf_clear, 1)
            def add(ig, q):
                if not isinstance(ig, int) or ig < IMAGE_GROUPS:
                    answers_add(an, pool, nc.gpsimd, ig, q)

            def turn(ig):
                for q in range(QT):
                    add(ig + (q + AHEAD) // QT, (q + AHEAD) % QT)
                    route_scatter(ro, pool, ig, q)
            for n in range(AHEAD):
                add(n // QT, n % QT)
            route_clear(ro, pool)
            turn(0)
            with pool.Fori(1, IMAGE_GROUPS - 2) as ig:
                turn(ig)
            turn(IMAGE_GROUPS - 2)
            turn(IMAGE_GROUPS - 1)
            route_finish(ro, pool)

        @block.tensor
        def _(pe):
            def three(out, wcols, k, mv_h, mv_l, start, stop):
                for n, (w, v) in enumerate(((r.gl, mv_h), (r.gh, mv_l), (r.gh, mv_h))):
                    ins = nc.tensor.matmul(out, w[0:k, wcols], v, start=start and n == 0, stop=stop and n == 2)
                return ins

            def up(ig, p):
                t, rho = divmod(p, ROWS)
                if rho == 0 and t < QT:
                    need(pe, xl_ready, QT * ig + t + 1)
                need(pe, y_copied, PAIRS * ig + last_user(p, 2, PAIRS) + 1)
                parts = []
                if t >= 1:
                    parts.append((2 * ROWS + rho, TPX + 1, t - 1) if t == QT else (rho, TPX, t - 1))
                if t < QT:
                    parts.append((ROWS + rho, TPX + 1, t))
                for j, (m, k, q) in enumerate(parts):
                    ins = three(ps_y[p % 2][0:PPX, :], up_w(m), k, xh[0:k, q, :], xl[0:k, q, :], j == 0, j == len(parts) - 1)
                ins.then_inc(y_raw, 1)

            def down(ig, p):
                need(pe, y_clip, PAIRS * ig + p + 1)
                t, rho = divmod(p, ROWS)
                for q, m in ((t - 1, ROWS + rho), (t, rho)):
                    if not 0 <= q < QT:
                        continue
                    rows = pixels(q)
                    if p == ROWS * q:
                        need(pe, z_added, QT * ig + last_user(q, 3, QT) + 1)
                    ins = nc.tensor.matmul(ps_z[q % 3][0:rows, :], r.down[0:PPX, m * TPX:m * TPX + rows], c[0:PPX, p % R, :],
                                           start=p == ROWS * q, stop=p == last_pair(q))
                ins.then_inc(down_done, 1)

            def step(it, n):
                for ig, p in pair(it, n):
                    up(ig, p)
                for ig, q in due(it, n, after(7)):
                    route_logits(ro, pe, ig, q)
                for ig, q in due(it, n, after(9)):
                    route_ranks(ro, pe, ig, q)
                for ig, p in pair(it, n - LAG):
                    down(ig, p)
                for ig, q in due(it, n, after(4)):
                    route_turn(ro, pe, ig, q)
            pe.wait_ge(bias_split, 1)
            turns(pe, step)
            route_count_all(ro, pe)

        @block.scalar
        def _(act):
            act.wait_ge(bias_in, 32)
            for q in range(QT):
                ins = nc.scalar.activation(xh[:, q], xf[:, 0], ACT.Copy)
            ins.then_inc(bias_high, 1)

            def high_x(ig, q):
                px = pixels(q)
                need(act, lnc.applied, QT * ig + q + 1)
                need(act, y_raw, PAIRS * (ig - 1) + last_pair(q) + 1)
                nc.scalar.activation(xh[0:px, q], xf[0:px, q % 2], ACT.Copy).then_inc(xh_ready, 1)

            def copy_y(ig, p):
                need(act, y_raw, PAIRS * ig + p + 1)
                need(act, y_leaky, PAIRS * ig + last_user(p, 2, PAIRS) + 1)
                nc.scalar.activation(a[0:PPX, p % 2, :], ps_y[p % 2][0:PPX, :], ACT.Copy).then_inc(y_copied, 1)

            def step(it, n):
                for ig, p in pair(it, n):
                    copy_y(ig, p)
                for ig, q in due(it, n, HIGH):
                    high_x(ig, q)
                for ig, q in due(it, n, ROOT):
                    norm_root(lnc, act, ig, q)
                for ig, q in due(it, n, after(2)):
                    norm_root(ro.norm, act, ig, q)
                for ig, q in due(it, n, after(4)):
                    route_copy_rows(ro, act, ig, q)
                for ig, q in due(it, n, after(5)):
                    route_copy_turned(ro, act, ig, q)
                for ig, q in due(it, n, after(8)):
                    route_exponent(ro, act, ig, q)
            turns(act, step)
            act.wait_ge(w_in, 32)
            nc.scalar.activation(wt.w1h[:], wt.w1f, ACT.Copy).then_inc(w_split, 1)

        @block.vector
        def _(dve):
            dve.wait_ge(bias_high, 1)
            for q in range(QT):
                ins = nc.vector.tensor_tensor(xl[:, q], xf[:, 0], xh[:, q].bitcast(F32), ALU.subtract)
            ins.then_inc(bias_split, 1)

            def measure(ig, q):
                g = QT * ig + q
                need(dve, an.added, g + 1, lnc.beat)
                norm_measure(lnc, dve, ig, q, r.x[0:pixels(q), bass.ds(g, 1)].rearrange("p a t c -> p (a t) c"))

            def normalise(ig, q):
                px = pixels(q)
                need(dve, xl_ready, QT * ig + last_user(q, 2, QT) + 1)
                if isinstance(ig, int) and ig == 0 and q < 2:
                    dve.wait_ge(bias_split, 1)
                x = r.x[0:px, bass.ds(QT * ig + q, 1)].rearrange("p a t c -> p (a t) c")
                norm_apply(lnc, dve, ig, q, xf[0:px, q % 2].rearrange("p (t c) -> p t c", c=P), x)

            def low_x(ig, q):
                px = pixels(q)
                need(dve, xh_ready, QT * ig + q + 1)
                nc.vector.tensor_tensor(xl[0:px, q], xf[0:px, q % 2], xh[0:px, q].bitcast(F32), ALU.subtract
                                        ).then_inc(xl_ready, 1)

            def leaky(ig, p):
                i, clamp = PAIRS * ig + p, 256.0 / GAIN
                need(dve, y_copied, i + 1)
                need(dve, down_done, PAIRS * ig + last_user(p, R, PAIRS) + 1)
                nc.vector.scalar_tensor_tensor(c[0:PPX, p % R, :], a[0:PPX, p % 2, :], 0.2, a[0:PPX, p % 2, :],
                                               ALU.mult, ALU.max).then_inc(y_leaky, 1)
                need(dve, y_leaky, i + 1)
                nc.vector.tensor_scalar(c[0:PPX, p % R, :], c[0:PPX, p % R, :], clamp, -clamp, ALU.min, ALU.max
                                        ).then_inc(y_clip, 1)

            def sum_z(ig, q):
                px, g = pixels(q), QT * ig + q
                need(dve, down_done, PAIRS * ig + last_pair(q) + 1)
                x = r.x[0:px, bass.ds(g, 1)].rearrange("p a t c -> p (a t c)")
                nc.vector.scalar_tensor_tensor(x, ps_z[q % 3][0:px, :], GAIN, x, ALU.mult, ALU.add).then_inc(z_added, 1)
                need(dve, z_added, g + 1, ro.norm.beat)
                norm_measure(ro.norm, dve, ig, q, r.x[0:px, bass.ds(g, 1)].rearrange("p a t c -> p (a t) c"))

            def step(it, n):
                for ig, p in pair(it, n):
                    leaky(ig, p)
                for ig, q in due(it, n, SCALE):
                    norm_scale(lnc, dve, ig, q)
                    normalise(ig, q)
                for ig, q in due(it, n, after(3)):
                    norm_scale(ro.norm, dve, ig, q)
                    route_normalise(ro, dve, ig, q)
                for ig, q in due(it, n, SPLIT):
                    low_x(ig, q)
                for ig, q in due(it, n, MEASURE):
                    measure(ig, q)
                for ig, q in due(it, n, after(1)):
                    sum_z(ig, q)
                for ig, q in due(it, n, after(7)):
                    route_pick(ro, dve, ig, q)
                for ig, q in due(it, n, after(9)):
                    route_place(ro, dve, ig, q)
            turns(dve, step)
            route_make_table(ro, dve)
            dve.wait_ge(w_split, 1)
            nc.vector.tensor_tensor(wt.w1l[:], wt.w1f, wt.w1h[:].bitcast(F32), ALU.subtract)


def combine_phase(nc, r, ys, out):
    with ExitStack() as ctx:
        sem = ctx.enter_context(stage_semaphores(nc, "m_"))
        an = Answers(nc, ctx, sem, r, ys, QT)
        stored = sem("stored")
        block = ctx.enter_context(nc.Block())

        @block.sync
        def _(sp):
            groups(sp, lambda ig, q: answers_load(an, sp, ig, q))

        @block.vector
        def _(dve):
            groups(dve, lambda ig, q: answers_add(an, dve, nc.vector, ig, q))

        @block.scalar
        def _(act):
            def store(ig, q):
                need(act, an.added, QT * ig + q + 1)
                act.dma_start(tile_of(out, ig, q), r.x[0:pixels(q), bass.ds(QT * ig + q, 1)].rearrange("p a t c -> p (a t) c")
                              ).then_inc(stored, 16)
            groups(act, store)
            act.wait_ge(stored, 16 * GROUPS)


def host_layouts(a):
    f32 = np.float32
    x = np.asarray(a["x"])
    io = {}
    xh = np.zeros((CGS, RPAD, IMAGES, SIDE, CIN), f32)
    xh[:, :SIDE] = x.reshape(IMAGES, CGS, CIN, SIDE, SIDE).transpose(1, 3, 0, 4, 2)
    io["xh"] = xh.reshape(P, NW, CIN)
    c = np.arange(P).reshape(P, 1, 1)
    kh, kw = np.arange(TAPS).reshape(1, TAPS, 1), np.arange(TAPS).reshape(1, 1, TAPS)
    idx = (c * 1337 + kh * 7919 + kw * 2971 + 3 * 104729) % 1024
    taps = np.asarray(a["L0_conv_codebook"])[idx].reshape(CGS, CIN, TAPS, TAPS)
    w0 = np.zeros((CIN, CGS, RPAD, TAPS, CGS, RPAD), f32)
    for ho in range(SIDE):
        for hi in range(max(0, ho - HALO), min(SIDE, ho + HALO + 1)):
            for g in range(CGS):
                w0[:, g, hi, :, g, ho] = taps[g, :, hi - ho + HALO, :]
    io["w0"] = w0.reshape(CIN, P, KLEN)
    b = np.asarray(a["L0_conv_bias"]).reshape(CGS, 1, CIN)
    io["bias0"] = np.ascontiguousarray(np.broadcast_to(b, (CGS, RPAD, CIN))).reshape(P, CIN)
    row = np.arange(P) % RPAD
    io["mean_w"] = ((row[:, None] == row[None, :]) & (row < SIDE)[:, None] & (row < SIDE)[None, :]).astype(f32) / f32(P)
    col = np.arange(NW) % SIDE
    io["check"] = np.stack([1.0 - 2.0 * ((row[:, None] + col) % 2), 1.0 - 2.0 * (col % 2) + 0 * row[:, None]], 1).astype(f32)
    sgn = 1.0 - 2.0 * (row % 2)
    io["osign"] = np.stack([-sgn, sgn], 1).astype(f32)
    io["wg0"] = np.asarray(a["L0_ffn_Wg"])
    io["wg1"] = np.asarray(a["L1_ffn_router_w"])
    io["w1_0"] = np.asarray(a["L0_ffn_W1"]).transpose(1, 0, 2)
    io["w2_0"] = np.asarray(a["L0_ffn_W2"]).reshape(EXPERTS, 4, P, P).transpose(2, 0, 1, 3)
    io["w1_1"] = np.concatenate([np.asarray(a["L1_ffn_w1"]), np.asarray(a["L1_ffn_w3"])], 2).transpose(1, 0, 2)
    io["w2_1"] = np.asarray(a["L1_ffn_w2"]).reshape(EXPERTS, 2, P, P).transpose(2, 0, 1, 3)
    p = np.arange(P)
    io["ident"] = np.eye(P, dtype=f32)
    io["before"] = (p[:, None] < p[None, :]).astype(f32)
    io["iota8"] = np.broadcast_to(np.arange(EXPERTS, dtype=f32), (P, IG, 2, EXPERTS)).reshape(P, CHOICES * EXPERTS)
    io["region"] = np.broadcast_to(np.arange(EXPERTS, dtype=f32) * REGION, (P, IG, EXPERTS)).reshape(P, IG * EXPERTS)
    io["block_no"] = np.arange(TABLE, dtype=f32).reshape(1, TABLE)
    io["dest"] = (np.arange(GROUPS)[:, None] * TPX * CHOICES + p[:, None, None] * CHOICES + np.arange(CHOICES)).astype(np.int32)
    blank = np.zeros((EXPERTS + SPARE, P, PAY), np.int32)
    blank[:, :, DEST] = ANSWERS + np.arange((EXPERTS + SPARE) * P).reshape(EXPERTS + SPARE, P)
    io["blank"] = blank[:EXPERTS].transpose(1, 0, 2).reshape(P, EXPERTS * PAY).view(np.float32)
    io["blank_rows"] = blank[EXPERTS:].reshape(SPARE * P, PAY).view(np.float32)
    fu, fd = np.asarray(a["L1_conv_up_filter"]), np.asarray(a["L1_conv_down_filter"])
    h, w = np.arange(P) // SIDE, np.arange(P) % SIDE
    e, j = np.arange(PPX) // UP, np.arange(PPX) % UP
    pix = (np.arange(P) < TPX)[:, None]
    fa, fb = np.zeros((P, N_UP, PPX), f32), np.zeros((P, N_UP, PPX), f32)
    mats = [(s, r, s == 1) for s in range(2) for r in range(ROWS)] + [(0, r, True) for r in range(4)]
    for m, (s, r, with_bias) in enumerate(mats):
        d = (ROWS if s == 0 else 0) + r - h[:, None]
        kr, kc = 2 * d + e[None, :], j[None, :] - 2 * w[:, None]
        fa[:, m] = np.where(pix & (kr >= 0) & (kr < FIR), fu[np.clip(kr, 0, FIR - 1)], 0)
        fb[:, m] = np.where(pix & (kc >= 0) & (kc < FIR), fu[np.clip(kc, 0, FIR - 1)], 0)
        if with_bias:
            fa[TPX, m], fb[TPX, m] = 1.0, 0.25
    io["up_a"], io["up_b"] = fa, fb
    e, j = np.arange(P) // UP, np.arange(P) % UP
    h, w = np.arange(TPX) // SIDE, np.arange(TPX) % SIDE
    pix = (np.arange(P) < PPX)[:, None]
    fa, fb = np.zeros((P, N_DOWN, TPX), f32), np.zeros((P, N_DOWN, TPX), f32)
    for m in range(N_DOWN):
        kr, kc = 2 * (m - h[None, :]) + e[:, None], j[:, None] - 2 * w[None, :]
        fa[:, m] = np.where(pix & (kr >= 0) & (kr < FIR), fd[np.clip(FIR - 1 - kr, 0, FIR - 1)], 0)
        fb[:, m] = np.where(pix & (kc >= 0) & (kc < FIR), fd[np.clip(FIR - 1 - kc, 0, FIR - 1)], 0)
    io["down_a"], io["down_b"] = fa, fb
    io["bias1"] = np.ascontiguousarray(np.broadcast_to(np.asarray(a["L1_conv_bias"]), (1, IG, P))).reshape(1, NC)
    return {k: np.ascontiguousarray(v) for k, v in io.items()}


def metaformer(nc, io, out):
    dram = lambda n, rows, cols: nc.dram_tensor(n, (rows, cols), F32).ap()
    x1 = nc.dram_tensor("x1", (SIDE, NW, P), F32).ap()
    xs, ys = dram("routed", EXPERTS * REGION + SPARE * P, PAY), dram("answers", ANSWERS + (EXPERTS + SPARE) * P, P)
    conv0_phase(nc, io, x1)
    with ExitStack() as ctx:
        r = Routing(nc, ctx)
        with ExitStack() as inner:
            wt = ExpertWeights(nc, inner, 0)
            route0_phase(nc, io, r, wt, xs, x1)
            expert_phase(nc, r, wt, 0, xs, ys)
        with ExitStack() as inner:
            wt = ExpertWeights(nc, inner, 1)
            conv1_phase(nc, io, r, wt, xs, ys)
            expert_phase(nc, r, wt, 1, xs, ys)
        combine_phase(nc, r, ys, out)


def kernel(**inputs):
    import concourse.bacc as bacc
    from concourse.bass_utils import run_bass_kernel_spmd

    nc = bacc.Bacc("TRN2", target_bir_lowering=False, num_devices=1)
    arrays = {f"in_{k}": v for k, v in host_layouts(inputs).items()}
    io = {k[3:]: nc.dram_tensor(k, v.shape, mybir.dt.from_np(v.dtype), kind="ExternalInput").ap() for k, v in arrays.items()}
    out = nc.dram_tensor("out", (TOKENS, P), F32, kind="ExternalOutput").ap()
    metaformer(nc, io, out)
    got = run_bass_kernel_spmd(nc, [arrays], core_ids=[0]).results[0]["out"]
    return got.reshape(IMAGES, SIDE, SIDE, P).transpose(0, 3, 1, 2)
```
